# Optimizing a Trainium2 kernel written in Bass

```python
import numpy as np
import jax
import jax.numpy as jnp

def _softmax(x, axis=-1):
    return jax.nn.softmax(x, axis=axis)

def _gelu(x):
    return jax.nn.gelu(x, approximate=True)

def _silu(x):
    return jax.nn.silu(x)

def _sigmoid(x):
    return jax.nn.sigmoid(x)

def _layernorm(x, axis=-1, eps=1e-05):
    m = jnp.mean(x, axis=axis, keepdims=True)
    v = jnp.var(x, axis=axis, keepdims=True)
    return (x - m) / jnp.sqrt(v + eps)

def _scatter_add(tgt, idx, src, axis=0):
    return tgt.at[idx].add(src)

def _segment_sum(src, seg, n):
    return jax.ops.segment_sum(src, seg, n)
kernel_name = 'mk_early_fusion_d1_tok_img1024_r4_f0baee'

def setup_inputs(seed: int=0):
    np.random.seed(seed)
    _w = jnp.asarray

    def _rec_inputs():
        import jax
        import jax.numpy as jnp
        _rk = jax.random.key(seed)
        x = -0.00016672 + 0.999947 * jax.random.normal(jax.random.fold_in(_rk, 1), (4, 3, 96, 96), jnp.float32)
        txt = 0.00222731 + 1.14264 * jax.random.normal(jax.random.fold_in(_rk, 2), (4, 512, 256), jnp.float32)
        return (x, txt)
    x, txt = _rec_inputs()

    def _L0_tok_setup():
        import jax, jax.numpy as jnp
        import numpy as np
        IN_CH, P, EMB, IMG_H, IMG_W = (3, 16, 256, 96, 96)
        N_PATCH = IMG_H // P * (IMG_W // P)
        key = jax.random.key(seed)
        k1, k2, k3, k4, k5 = jax.random.split(key, 5)
        x = jax.random.normal(k1, (64, IN_CH, IMG_H, IMG_W), dtype=jnp.float32)
        W = jax.random.normal(k2, (P * P * IN_CH, EMB), dtype=jnp.float32) * 0.02
        b = jax.random.normal(k3, (EMB,), dtype=jnp.float32) * 0.02
        cls_token = jax.random.normal(k4, (1, 1, EMB), dtype=jnp.float32)
        pos_emb = jax.random.normal(k5, (N_PATCH + 1, EMB), dtype=jnp.float32)
        return {'x': x, 'W': W, 'b': b, 'cls_token': cls_token, 'pos_emb': pos_emb}
    _L0_tok_all = _L0_tok_setup()
    _L0_tok_in = {k: v for k, v in _L0_tok_all.items() if k in ('W', 'b', 'cls_token', 'pos_emb')}
    del _L0_tok_all

    def _L0_attn_setup():
        import math
        import jax, jax.numpy as jnp
        import numpy as np
        B, T, C, H, DQK, DV = (2, 512, 256, 16, 64, 64)
        key = jax.random.key(seed)
        ks = jax.random.split(key, 5)
        x = jax.random.normal(ks[0], (B, T, C), dtype=jnp.float32)
        w_q = jax.random.normal(ks[1], (H, DQK, C), dtype=jnp.float32) / math.sqrt(C)
        w_k = jax.random.normal(ks[2], (H, DQK, C), dtype=jnp.float32) / math.sqrt(C)
        w_v = jax.random.normal(ks[3], (H, DV, C), dtype=jnp.float32) / math.sqrt(C)
        w_o = jax.random.normal(ks[4], (DV * H, C), dtype=jnp.float32) / math.sqrt(C)
        return {'x': x, 'w_q': w_q, 'w_k': w_k, 'w_v': w_v, 'w_o': w_o}
    _L0_attn_all = _L0_attn_setup()
    _L0_attn_in = {k: v for k, v in _L0_attn_all.items() if k in ('w_q', 'w_k', 'w_v', 'w_o')}
    del _L0_attn_all

    def _L0_ffn_setup():
        import jax, jax.numpy as jnp
        import numpy as np
        TOP_K = 2
        key = jax.random.key(seed)
        ks = jax.random.split(key, 5)
        B, T, D, E, F = (2, 512, 256, 8, 512)
        scale_d = 1.0 / np.sqrt(D)
        scale_f = 1.0 / np.sqrt(F)
        return {'x': jax.random.normal(ks[0], (B, T, D), jnp.float32), 'kernel_router_DE': jax.random.normal(ks[1], (D, E), jnp.float32) * scale_d, 'kernel_gating_EDF': jax.random.normal(ks[2], (E, D, F), jnp.float32) * scale_d, 'kernel_up_EDF': jax.random.normal(ks[3], (E, D, F), jnp.float32) * scale_d, 'kernel_down_EFD': jax.random.normal(ks[4], (E, F, D), jnp.float32) * scale_f}
    _L0_ffn_all = _L0_ffn_setup()
    _L0_ffn_in = {k: v for k, v in _L0_ffn_all.items() if k in ('kernel_router_DE', 'kernel_gating_EDF', 'kernel_up_EDF', 'kernel_down_EFD')}
    del _L0_ffn_all
    return {'x': x, 'txt': txt, 'L0_tok_W': _L0_tok_in['W'], 'L0_tok_b': _L0_tok_in['b'], 'L0_tok_cls_token': _L0_tok_in['cls_token'], 'L0_tok_pos_emb': _L0_tok_in['pos_emb'], 'L0_attn_w_q': _L0_attn_in['w_q'], 'L0_attn_w_k': _L0_attn_in['w_k'], 'L0_attn_w_v': _L0_attn_in['w_v'], 'L0_attn_w_o': _L0_attn_in['w_o'], 'L0_ffn_kernel_router_DE': _L0_ffn_in['kernel_router_DE'], 'L0_ffn_kernel_gating_EDF': _L0_ffn_in['kernel_gating_EDF'], 'L0_ffn_kernel_up_EDF': _L0_ffn_in['kernel_up_EDF'], 'L0_ffn_kernel_down_EFD': _L0_ffn_in['kernel_down_EFD']}

def reference(x, txt, L0_tok_W, L0_tok_b, L0_tok_cls_token, L0_tok_pos_emb, L0_attn_w_q, L0_attn_w_k, L0_attn_w_v, L0_attn_w_o, L0_ffn_kernel_router_DE, L0_ffn_kernel_gating_EDF, L0_ffn_kernel_up_EDF, L0_ffn_kernel_down_EFD):
    import jax
    import jax.numpy as jnp

    def _L0_tok_ref(x, W, b, cls_token, pos_emb):
        import jax, jax.numpy as jnp
        import numpy as np
        IN_CH, P, EMB, IMG_H, IMG_W = (3, 16, 256, 96, 96)
        N_PATCH = IMG_H // P * (IMG_W // P)
        B, C, H, Wd = x.shape
        p = P
        xp = x.reshape(B, C, H // p, p, Wd // p, p)
        xp = jnp.transpose(xp, (0, 2, 4, 3, 5, 1)).reshape(B, -1, p * p * C)
        tok = jnp.einsum('bnf,fe->bne', xp, W) + b
        cls = jnp.broadcast_to(cls_token, (B, 1, tok.shape[-1]))
        out = jnp.concatenate([cls, tok], axis=1) + pos_emb
        return out

    def _L0_attn_ref(x, w_q, w_k, w_v, w_o):
        import math
        import jax, jax.numpy as jnp
        import numpy as np
        B, T, C, H, DQK, DV = (2, 512, 256, 16, 64, 64)
        n, t, c = x.shape
        q = jnp.einsum('ntc,hdc->nhtd', x, w_q)
        k = jnp.einsum('ntc,hdc->nhtd', x, w_k)
        v = jnp.einsum('ntc,hdc->nhtd', x, w_v)
        scale = 1.0 / math.sqrt(w_q.shape[1])
        a = jnp.einsum('nhtd,nhsd->nhts', q, k) * scale
        causal = jnp.arange(t)[:, None] < jnp.arange(t)[None, :]
        a = jnp.where(causal[None, None, :, :], -jnp.inf, a)
        a = jax.nn.softmax(a, axis=3)
        y = jnp.einsum('nhts,nhsd->nthd', a, v).reshape(n, t, -1)
        return y @ w_o

    def _L0_ffn_ref(x, kernel_router_DE, kernel_gating_EDF, kernel_up_EDF, kernel_down_EFD):
        import jax, jax.numpy as jnp
        import numpy as np
        TOP_K = 2
        E = kernel_router_DE.shape[-1]
        x = x.astype(jnp.float32)
        router_logits_BTE = jnp.einsum('BTD,DE->BTE', x, kernel_router_DE)
        probs_BTE = jax.nn.softmax(router_logits_BTE.astype(jnp.float32), axis=-1)
        weights_BTX, indices_BTX = jax.lax.top_k(probs_BTE, TOP_K)
        norm_weights_BTX = jax.nn.softmax(weights_BTX, axis=-1)
        one_hot_BTXE = jax.nn.one_hot(indices_BTX, num_classes=E, dtype=jnp.float32)
        full_weights_BTE = jnp.sum(one_hot_BTXE * norm_weights_BTX[..., None], axis=2)
        gating_BTEF = jnp.einsum('BTD,EDF->BTEF', x, kernel_gating_EDF)
        fuse_BTEF = jax.nn.silu(gating_BTEF) * jnp.einsum('BTD,EDF->BTEF', x, kernel_up_EDF)
        down_BTED = jnp.einsum('BTEF,EFD->BTED', fuse_BTEF, kernel_down_EFD)
        out_BTD = jnp.einsum('BTED,BTE->BTD', down_BTED, full_weights_BTE)
        return out_BTD.astype(jnp.float32)
    h = _L0_tok_ref(x, L0_tok_W, L0_tok_b, L0_tok_cls_token, L0_tok_pos_emb)
    h = jnp.concatenate([h, txt], axis=1)
    h = h + _L0_attn_ref(_layernorm(h, axis=-1), L0_attn_w_q, L0_attn_w_k, L0_attn_w_v, L0_attn_w_o)
    h = h + _L0_ffn_ref(_layernorm(h, axis=-1), L0_ffn_kernel_router_DE, L0_ffn_kernel_gating_EDF, L0_ffn_kernel_up_EDF, L0_ffn_kernel_down_EFD)
    return h

_drawn_inputs = setup_inputs


def setup_inputs(seed=0):
    import zlib

    import numpy as np

    out = dict(_drawn_inputs(seed))
    spreads = {}
    factors = {}
    for name, (base, spread) in spreads.items():
        noise = np.random.default_rng([zlib.crc32(name.encode()), seed]).standard_normal(out[name].shape)
        drawn = base * np.exp(spread * noise) if base else spread * noise
        out[name] = jnp.asarray(drawn.astype(out[name].dtype))
    for name, factor in factors.items():
        out[name] = (out[name] * factor).astype(out[name].dtype)
    return out
```

```python
from contextlib import ExitStack

import concourse.bass as bass
from concourse import mybir

F32 = mybir.dt.float32
F32R = mybir.dt.float32r
ALU = mybir.AluOpType
ACT = mybir.ActivationFunctionType
AX = mybir.AxisListType

B, CH, IMG, P = 4, 3, 96, 16
C = 256
CC = C // 128
G = IMG // P
NP = G * G
TXT = 512
T0 = NP + 1
NT = 1 + TXT // 128
T = T0 + TXT
TP = 552
HT = TP // 2
H, D = 16, 64
HD = H * D
NPAIR = H // 2
E, F = 8, 512
FT = F // 128
LN_EPS = 1e-5
Q_SCALE = -1.0 / D ** 0.5
MASKED = 1e30

SIZE = [T0] + [128] * (NT - 1)
START = [0] + [T0 + 128 * i for i in range(NT - 1)]
SEEN = [START[i] + SIZE[i] for i in range(NT)]
P_AT = [sum(SEEN[:i]) for i in range(NT)]
P_LEN = P_AT[-1] + TP

NTOK = B * T
REST = B * TXT
CHUNKS = [(0, 512), (512, 1024), (1024, 1536), (1536, 1920), (1920, NTOK)]
X_ROWS = 3 * T0
DOWN = [(128 * k, 128) for k in range(B * (NT - 1))] + [(REST, X_ROWS), (REST + X_ROWS, T0)]
ND = len(DOWN)


def chunk_tiles(c):
    lo, hi = CHUNKS[c]
    return [k for k, (at, _) in enumerate(DOWN) if lo <= at < hi]


def units_of_a_batch():
    units = [("xT", i) for i in range(NT)]
    units += [("V", i, half) for i in range(NT) for half in range(2)]
    units += [("Q", 0), ("K", 0)] + [("S", 0, i) for i in (4, 3, 2, 1, 0)]
    for p in range(NPAIR - 1):
        units += [("Q", p + 1), ("K", p + 1)] + [("S", p + 1, i) for i in (4, 3, 2, 1, 0)]
    units += [("O", i) for i in range(NT)]
    units += [("x2T", i) for i in range(NT)]
    banks, turn = {}, 0
    for u in units:
        if u[0] == "S":
            i = u[2]
            banks[u] = [0, 1, 2, 3] if i == 4 else [i % 2, 2 + i % 2]
        elif u[0] in "QK":
            banks[u] = [0, 1] if u[0] == "Q" else [2, 3]
        else:
            banks[u] = [turn % 4]
            turn += 1
    number = {u: n for n, u in enumerate(units)}
    blocker, last = {}, {}
    for n, u in enumerate(units):
        before = [last[b] for b in banks[u] if b in last]
        blocker[u] = max(before) + 1 if before else 0
        for b in banks[u]:
            last[b] = n
    freed, count = {}, 1
    for u in units:
        count += 2 if u[0] == "S" else 1
        freed[u] = count
    blocker = {u: freed[units[n - 1]] if n else 0 for u, n in blocker.items()}
    return units, number, banks, blocker, freed


def fusion_block_kernel(nc, x, txt, tok_w, tok_b, cls_token, pos_emb, w_q, w_k, w_v, w_o,
                        w_router, w_gate, w_up, w_down, out):
    UNITS, UNIT, BANKS, BLOCKER, FREED = units_of_a_batch()
    NU, NF = len(UNITS), FREED[UNITS[-1]] - 1
    HI_UNITS = [u for u in UNITS if u[0] in ("xT", "Q", "K")]
    HI = {u: n for n, u in enumerate(HI_UNITS)}
    NS = NPAIR * NT * 2
    S_NO = {(p, i, h): (p * NT + (4 - i)) * 2 + h
            for p in range(NPAIR) for i in range(NT) for h in range(2)}

    ctx = ExitStack()
    with ctx:
        def sem(name):
            return ctx.enter_context(nc.semaphore(name))

        def keep(name, shape, dt=F32):
            return ctx.enter_context(nc.sbuf_tensor(name, shape, dt))

        acc = keep("acc", [128, B * (NT - 1), C])
        first = keep("first", [T0, B, C])
        x2T = keep("x2T", [128, CC, NTOK])
        ident = keep("ident", [128, 128])
        work = ctx.enter_context(nc.psum_tensor("work", [128, 4, 512], F32))
        turned = [ctx.enter_context(nc.psum_tensor(f"turned{h}", [128, 512], F32)) for h in range(2)]
        y_text = ctx.enter_context(nc.psum_tensor("y_text", [128, 512], F32))
        y_first = ctx.enter_context(nc.psum_tensor("y_first", [128, 512], F32))

        with ExitStack() as one:
            def sb(name, shape, dt=F32):
                return one.enter_context(nc.sbuf_tensor(name, shape, dt))

            whi = sb("whi", [128, 3, CC, HD], F32R)
            wlo = sb("wlo", [128, 3, CC, HD], F32R)
            wo = sb("wo", [128, NPAIR, C])
            xhi = sb("xhi", [128, CC, TP], F32R)
            xlo = sb("xlo", [128, CC, TP], F32R)
            v = sb("v", [128, NT, HD])
            prob = sb("prob", [128, 2, 2, P_LEN])
            probT = sb("probT", [128, 2, 2, 512])
            probT0 = sb("probT0", [T0, 2, T0])
            yT = sb("yT", [128, NPAIR, TP])
            qk_hi = sb("qk_hi", [128, 2, 2, TP], F32R)
            qk_lo = sb("qk_lo", [128, 2, 2, TP], F32R)
            xhat = sb("xhat", [128, 2, C])
            mask = sb("mask", [128, TP + START[-1]])
            low = sb("low", [128, 2, NT, 2])
            total = sb("total", [128, 2, NT, 2])
            share = sb("share", [128, 2, NT, 2])
            stats = sb("stats", [128, NT, 6])
            mean_var = sb("mean_var", [128, NT, 2])
            var_eps = sb("var_eps", [128, NT])
            rstd = sb("rstd", [128, NT])
            minus_half = sb("minus_half", [128, NT])
            extra = sb("extra", [T0, 2, C])
            pflat = prob[:, :, :, :].rearrange("p a h n -> p (a h n)")
            raw = [pflat[:, 0:8 * C].rearrange("p (r c) -> p r c", r=8),
                   pflat[:, 8 * C:16 * C].rearrange("p (r c) -> p r c", r=8),
                   yT[:, :, :].rearrange("p a n -> p (a n)")[:, 0:8 * C].rearrange("p (r c) -> p r c", r=8)]
            tokw = v[0:CH * P, :, :].rearrange("p a n -> p (a n)")[:, 0:P * C].rearrange("p (d e) -> p d e", d=P)
            COLS = 64 + T0
            px = x2T[0:CH * P, :, :].rearrange("p a n -> p (a n)")[:, 0:2 * COLS * P].rearrange(
                "p (g s d) -> p g s d", g=2, d=P)

            w_in = [sem(f"w_in{m}") for m in range(3)]
            wo_in, tokw_in, px_in, extra_in, txt_in = (sem(n) for n in ("wo_in", "tokw_in", "px_in", "extra_in", "txt_in"))
            made = sem("made")
            px_zero = sem("px_zero")
            pads = sem("pads")
            w_turned, w_hi, w_lo = sem("w_turned"), sem("w_hi"), sem("w_lo")
            patch_ready, patch_done, extra_done = sem("patch_ready"), sem("patch_done"), sem("extra_done")
            unit_ready, unit_free = sem("unit_ready"), sem("unit_free")
            hi_done = sem("hi_done")
            stats_done, aggr_done, eps_done, rstd_done, xhat_done = (
                sem(n) for n in ("stats_done", "aggr_done", "eps_done", "rstd_done", "xhat_done"))
            h2_done = sem("h2_done")
            exp_done, share_done, norm_done = (
                sem(n) for n in ("exp_done", "share_done", "norm_done"))
            turn_ready = [sem(f"turn_ready{h}") for h in range(2)]
            turn_done = [sem(f"turn_done{h}") for h in range(2)]
            pv_done, y_ready, y_done = sem("pv_done"), sem("y_ready"), sem("y_done")
            passed_dve, passed_pe = sem("passed_dve"), sem("passed_pe")
            NTURN = NT + 1

            with nc.Block() as block:
                W_UNITS = [(m, c, half) for m in range(3) for c in range(CC) for half in range(2)]

                @block.sync
                def _(sp):
                    for m, w in enumerate((w_q, w_k, w_v)):
                        sp.dma_start(raw[m], w.rearrange("h d c -> (h d) c").rearrange(
                            "(r p) c -> p r c", p=128)).then_inc(w_in[m], 16)
                    for ch in range(CH):
                        sp.dma_start(tokw[ch * P:(ch + 1) * P], tok_w.rearrange(
                            "(y x c) e -> c y x e", y=P, c=CH)[ch]).then_inc(tokw_in, 16)
                    sp.wait_ge(px_zero, 1)
                    for b in range(B):
                        g, side = b // 2, b % 2
                        for ch in range(CH):
                            sp.dma_start(
                                px[ch * P:(ch + 1) * P, g, 64 * side + 1:64 * side + T0, :].rearrange(
                                    "y (r q) d -> y r (q d)", r=G),
                                x[b, ch].rearrange("(r y) w -> y r w", y=P)).then_inc(px_in, 16)
                    sp.dma_start(extra[:, 0, :], pos_emb).then_inc(extra_in, 16)
                    sp.dma_start(extra[0:1, 1, :], cls_token.rearrange("a b e -> (a b) e")).then_inc(extra_in, 16)
                    sp.dma_start(extra[1:T0, 1, :], tok_b.rearrange("(a e) -> a e", a=1).to_broadcast([NP, C])
                                 ).then_inc(extra_in, 16)
                    sp.dma_start(wo[:, :, :], w_o.rearrange("(r p) c -> p r c", p=128)).then_inc(wo_in, 16)
                    for b in range(B):
                        sp.dma_start(acc[:, b * (NT - 1):(b + 1) * (NT - 1), :], txt[b].rearrange(
                            "(r p) c -> p r c", p=128)).then_inc(txt_in, 16)

                @block.gpsimd
                def _(pool):
                    nc.gpsimd.memset(ident[:, :], 1.0).then_inc(made, 1)
                    nc.gpsimd.memset(mask[:, :], 0.0).then_inc(made, 1)
                    nc.gpsimd.memset(minus_half[:, :], -0.5).then_inc(made, 1)
                    pool.wait_ge(made, 3)
                    nc.gpsimd.affine_select(out=ident[:, :], in_=ident[:, :], pattern=[[-1, 128]],
                                            compare_op=ALU.is_equal, fill=0.0, base=0,
                                            channel_multiplier=1).then_inc(made, 1)
                    nc.gpsimd.affine_select(out=mask[:, :], in_=mask[:, :], pattern=[[-1, TP + START[-1]]],
                                            compare_op=ALU.is_ge, fill=MASKED, base=START[-1],
                                            channel_multiplier=1).then_inc(made, 1)
                    with pool.Fori(0, B) as b:
                        def rstd_of_all(n):
                            pool.wait_ge(eps_done, b * 2 + n + 1)
                            nc.gpsimd.tensor_tensor(rstd[:, :], var_eps[:, :], minus_half[:, :],
                                                    ALU.pow).then_inc(rstd_done, 1)

                        rstd_of_all(0)
                        for p in range(NPAIR):
                            for i in (4, 3, 2, 1, 0):
                                for h in range(2):
                                    pool.wait_ge(share_done, b * NPAIR * NT + p * NT + (4 - i) + 1)
                                    rows = prob[0:SIZE[i], p % 2, h, P_AT[i]:P_AT[i] + SEEN[i]]
                                    nc.gpsimd.tensor_tensor(
                                        rows, rows, share[0:SIZE[i], p % 2, i, h:h + 1].to_broadcast(
                                            [SIZE[i], SEEN[i]]), ALU.mult).then_inc(norm_done, 1)
                        rstd_of_all(1)

                @block.tensor
                def _(pe):
                    pe.wait_ge(made, 5)
                    for n, (m, c, half) in enumerate(W_UNITS):
                        if n % 4 == 0 and c == 0 and half == 0:
                            pe.wait_ge(w_in[m], 16)
                        if n >= 4:
                            pe.wait_ge(w_lo, n - 3)
                        for r in range(4):
                            mm = nc.tensor.transpose(work[:, n % 4, r * 128:(r + 1) * 128],
                                                     raw[m][:, 4 * half + r, c * 128:(c + 1) * 128], ident[:, :])
                        mm.then_inc(w_turned, 1)
                    pe.wait_ge(tokw_in, 16 * CH)
                    pe.wait_ge(px_in, 16 * CH * B)
                    for g in range(2):
                        for d in range(P):
                            mm = nc.tensor.matmul(turned[g][0:COLS, 0:C], px[:, g, :, d], tokw[:, d, :],
                                                  start=(d == 0), stop=(d == P - 1))
                        mm.then_inc(patch_ready, 1)
                    pe.wait_ge(w_lo, len(W_UNITS))
                    pe.wait_ge(patch_done, B)
                    pe.wait_ge(pads, 2)

                    with pe.Fori(0, B) as b:
                        pe.wait_ge(unit_free, b * NF + 1)

                        def claim(u, after=None):
                            n = max(BLOCKER[u], FREED[after] if after else 0)
                            if n:
                                pe.wait_ge(unit_free, b * NF + n)

                        def three(dst, a, m, first_, last_):
                            nc.tensor.matmul(dst, a[0], m[0], start=first_, stop=False)
                            nc.tensor.matmul(dst, a[0], m[1], start=False, stop=False)
                            return nc.tensor.matmul(dst, a[1], m[0], start=False, stop=last_)

                        def turn_x(kind, i, n):
                            u = (kind, i)
                            claim(u)
                            pe.wait_ge(xhat_done, b * 2 * NT + n * NT + i + 1)
                            if i == 0:
                                pe.sem_inc(passed_pe, 1)
                            for c in range(CC):
                                mm = nc.tensor.transpose(work[:, BANKS[u][0], c * 128:c * 128 + SIZE[i]],
                                                         xhat[0:SIZE[i], i % 2, c * 128:(c + 1) * 128],
                                                         ident[0:SIZE[i], 0:SIZE[i]])
                            mm.then_inc(unit_ready, 1)

                        def values(i, half):
                            u = ("V", i, half)
                            claim(u, ("xT", i))
                            cols = slice(START[i], START[i] + SIZE[i])
                            n = slice(half * 512, half * 512 + 512)
                            for c in range(CC):
                                mm = three(work[0:SIZE[i], BANKS[u][0], :], (xhi[:, c, cols], xlo[:, c, cols]),
                                           (whi[:, 2, c, n], wlo[:, 2, c, n]), c == 0, c == CC - 1)
                            mm.then_inc(unit_ready, 1)

                        def project(kind, p):
                            u = (kind, p)
                            m = "QK".index(kind)
                            claim(u, ("xT", NT - 1))
                            rows = slice(p * 128, p * 128 + 128)
                            for s in range(2):
                                n = slice(s * HT, s * HT + HT)
                                for c in range(CC):
                                    mm = three(work[:, BANKS[u][s], 0:HT], (whi[:, m, c, rows], wlo[:, m, c, rows]),
                                               (xhi[:, c, n], xlo[:, c, n]), c == 0, c == CC - 1)
                            mm.then_inc(unit_ready, 1)

                        def scores(p, i):
                            u = ("S", p, i)
                            claim(u, ("K", p))
                            if i == 0:
                                pe.sem_inc(passed_pe, 1)
                            cols = slice(START[i], START[i] + SIZE[i])
                            n = SEEN[i] + SEEN[i] % 2
                            parts = [(0, HT), (HT, TP)] if i == 4 else [(0, max(n, 256) if i else n)]
                            for s, (lo, hi) in enumerate(parts):
                                for a, m in ((qk_hi, qk_hi), (qk_hi, qk_lo), (qk_lo, qk_hi)):
                                    for h in range(2):
                                        rows = slice(64 * h, 64 * h + 64)
                                        bank = 2 * h + s if i == 4 else BANKS[u][h]
                                        mm = nc.tensor.matmul(work[0:SIZE[i], bank, 0:hi - lo],
                                                              a[rows, p % 2, 0, cols], m[rows, p % 2, 1, lo:hi],
                                                              start=(a is qk_hi and m is qk_hi),
                                                              stop=(a is qk_lo))
                            mm.then_inc(unit_ready, 1)

                        def turn_p(p, j):
                            for h in range(2):
                                n = p * NTURN + j
                                pe.wait_ge(turn_done[h], 1 + b * NPAIR * NTURN + n)
                                pe.wait_ge(norm_done, b * NS + S_NO[p, j if j else 1, h] + 1)
                                if j == 0:
                                    pe.sem_inc(passed_pe, 1)
                                for i in range(max(j, 1), NT):
                                    at = (i - max(j, 1)) * 128
                                    mm = nc.tensor.transpose(
                                        turned[h][0:SIZE[j], at:at + 128],
                                        prob[:, p % 2, h, P_AT[i] + START[j]:P_AT[i] + START[j] + SIZE[j]],
                                        ident[:, :])
                                mm.then_inc(turn_ready[h], 1)

                        def turn_p0(p):
                            for h in range(2):
                                pe.wait_ge(turn_done[h], 1 + b * NPAIR * NTURN + p * NTURN + NT)
                                pe.wait_ge(norm_done, b * NS + S_NO[p, 0, h] + 1)
                                pe.sem_inc(passed_pe, 1)
                                nc.tensor.transpose(turned[h][0:T0, 0:T0], prob[0:T0, p % 2, h, 0:T0],
                                                    ident[0:T0, 0:T0]).then_inc(turn_ready[h], 1)

                        def weigh(p, j):
                            if j == 0:
                                pe.wait_ge(y_done, 1 + b * NPAIR + p)
                            at = START[max(j, 1)] - T0
                            for h in range(2):
                                pe.wait_ge(turn_done[h], 1 + b * NPAIR * NTURN + p * NTURN + j + 1)
                            if j == 0:
                                pe.sem_inc(passed_pe, 1)
                            for h in range(2):
                                cols = slice(p * 128 + 64 * h, p * 128 + 64 * h + 64)
                                mm = nc.tensor.matmul(y_text[64 * h:64 * h + 64, at:512], v[0:SIZE[j], j, cols],
                                                      probT[0:SIZE[j], j % 2, h, 0:512 - at],
                                                      start=(j == 0), stop=(j == NT - 1))
                            mm.then_inc(pv_done, 1)

                        def weigh_first(p):
                            for h in range(2):
                                pe.wait_ge(turn_done[h], 1 + b * NPAIR * NTURN + (p + 1) * NTURN)
                            pe.sem_inc(passed_pe, 1)
                            for h in range(2):
                                cols = slice(p * 128 + 64 * h, p * 128 + 64 * h + 64)
                                mm = nc.tensor.matmul(y_first[64 * h:64 * h + 64, 0:T0], v[0:T0, 0, cols],
                                                      probT0[:, h, :], start=True, stop=True)
                            mm.then_inc(y_ready, 1)

                        for i in range(NT):
                            turn_x("xT", i, 0)
                        for i in range(NT):
                            for half in range(2):
                                values(i, half)
                        project("Q", 0)
                        project("K", 0)
                        for i in (4, 3, 2, 1, 0):
                            scores(0, i)
                        for p in range(NPAIR):
                            more = p + 1 < NPAIR
                            if more:
                                project("Q", p + 1)
                                project("K", p + 1)
                            turn_p(p, 0)
                            turn_p(p, 1)
                            for j in range(NT):
                                if more:
                                    scores(p + 1, 4 - j)
                                weigh(p, j)
                                if j + 2 < NT:
                                    turn_p(p, j + 2)
                                elif j + 2 == NT:
                                    turn_p0(p)
                            weigh_first(p)

                        for i in range(NT):
                            u = ("O", i)
                            claim(u)
                            pe.wait_ge(y_done, 1 + b * NPAIR + NPAIR)
                            if i == 0:
                                pe.wait_ge(wo_in, 16)
                            for p in range(NPAIR):
                                mm = nc.tensor.matmul(work[0:SIZE[i], BANKS[u][0], 0:C],
                                                      yT[:, p, START[i]:START[i] + SIZE[i]], wo[:, p, :],
                                                      start=(p == 0), stop=(p == NPAIR - 1))
                            mm.then_inc(unit_ready, 1)
                        for i in range(NT):
                            turn_x("x2T", i, 1)

                @block.scalar
                def _(act):
                    for n, (m, c, half) in enumerate(W_UNITS):
                        act.wait_ge(w_turned, n + 1)
                        nc.scalar.activation(whi[:, m, c, half * 512:(half + 1) * 512], work[:, n % 4, :], ACT.Copy,
                                             scale=Q_SCALE if m == 0 else 1.0).then_inc(w_hi, 1)
                    act.sem_inc(turn_done[0], 1)
                    act.sem_inc(y_done, 1)

                    with act.Fori(0, B) as b:
                        act.wait_ge(unit_free, b * NF + 1)

                        def upper(u, dst, src):
                            act.wait_ge(unit_ready, b * NU + UNIT[u] + 1)
                            nc.scalar.activation(dst, src, ACT.Copy).then_inc(hi_done, 1)

                        def upper_qk(kind, p):
                            u = (kind, p)
                            k = "QK".index(kind)
                            upper(u, qk_hi[:, p % 2, k, :].rearrange("p (s n) -> p s n", s=2),
                                  work[:, BANKS[u][0]:BANKS[u][0] + 2, 0:HT])

                        def expo(p, i):
                            for h in range(2):
                                act.wait_ge(unit_free, b * NF + FREED["S", p, i] - 1 + h)
                                rows = prob[0:SIZE[i], p % 2, h, P_AT[i]:P_AT[i] + SEEN[i]]
                                nc.scalar.activation(rows, rows, ACT.Exp, scale=-1.0,
                                                     bias=low[0:SIZE[i], p % 2, i, h:h + 1],
                                                     accum_out=total[0:SIZE[i], p % 2, i, h:h + 1]
                                                     ).then_inc(exp_done, 1)

                        def take_turned(p, j):
                            act.wait_ge(turn_ready[0], b * NPAIR * NTURN + p * NTURN + j + 1)
                            if j >= 2:
                                act.wait_ge(pv_done, b * NPAIR * NT + p * NT + j - 1)
                            elif p:
                                act.wait_ge(pv_done, b * NPAIR * NT + p * NT)
                            w = 512 - (START[max(j, 1)] - T0)
                            nc.scalar.activation(probT[0:SIZE[j], j % 2, 0, 0:w], turned[0][0:SIZE[j], 0:w],
                                                 ACT.Copy).then_inc(turn_done[0], 1)

                        for i in range(NT):
                            u = ("xT", i)
                            upper(u, xhi[:, :, START[i]:START[i] + SIZE[i]],
                                  work[:, BANKS[u][0], 0:CC * 128].rearrange("p (c n) -> p c n", c=CC)[:, :, 0:SIZE[i]])
                        upper_qk("Q", 0)
                        upper_qk("K", 0)
                        for i in (4, 3, 2, 1, 0):
                            expo(0, i)
                        for p in range(NPAIR):
                            more = p + 1 < NPAIR
                            if more:
                                upper_qk("Q", p + 1)
                                upper_qk("K", p + 1)
                            take_turned(p, 0)
                            take_turned(p, 1)
                            for j in range(NT):
                                if more:
                                    expo(p + 1, 4 - j)
                                if j + 2 < NT:
                                    take_turned(p, j + 2)
                                elif j + 2 == NT:
                                    act.wait_ge(turn_ready[0], b * NPAIR * NTURN + (p + 1) * NTURN)
                                    if p:
                                        act.wait_ge(y_ready, b * NPAIR + p)
                                    nc.scalar.activation(probT0[:, 0, :], turned[0][0:T0, 0:T0],
                                                         ACT.Copy).then_inc(turn_done[0], 1)
                            act.wait_ge(y_ready, b * NPAIR + p + 1)
                            nc.scalar.activation(yT[:, p, 0:T0], y_first[:, 0:T0], ACT.Copy)
                            nc.scalar.activation(yT[:, p, T0:T], y_text[:, :], ACT.Copy).then_inc(y_done, 1)

                @block.vector
                def _(dve):
                    nc.vector.memset(px, 0.0).then_inc(px_zero, 1)
                    for t in (xhi, xlo):
                        nc.vector.memset(t[:, :, T:TP].bitcast(F32), 0.0).then_inc(pads, 1)
                    nc.vector.memset(var_eps[:, :], 1.0).then_inc(pads, 1)
                    for n, (m, c, half) in enumerate(W_UNITS):
                        dve.wait_ge(w_hi, n + 1)
                        dst = wlo[:, m, c, half * 512:(half + 1) * 512]
                        top = whi[:, m, c, half * 512:(half + 1) * 512].bitcast(F32)
                        nc.vector.scalar_tensor_tensor(out=dst, in0=work[:, n % 4, :], scalar=Q_SCALE if m == 0 else 1.0,
                                                       in1=top, op0=ALU.mult, op1=ALU.subtract).then_inc(w_lo, 1)
                    dve.wait_ge(extra_in, 48)
                    nc.vector.tensor_tensor(extra[:, 0, :], extra[:, 0, :], extra[:, 1, :], ALU.add).then_inc(extra_done, 1)
                    dve.wait_ge(extra_done, 1)
                    for b in range(B):
                        dve.wait_ge(patch_ready, b // 2 + 1)
                        at = 64 * (b % 2)
                        nc.vector.tensor_tensor(first[:, b, :], turned[b // 2][at:at + T0, 0:C], extra[:, 0, :],
                                                ALU.add).then_inc(patch_done, 1)
                    dve.wait_ge(patch_done, B)
                    dve.wait_ge(txt_in, 16 * B)
                    dve.wait_ge(made, 5)
                    dve.wait_ge(pads, 3)
                    dve.sem_inc(unit_free, 1)
                    dve.sem_inc(turn_done[1], 1)

                    with dve.Fori(0, B) as b:
                        dve.wait_ge(unit_free, b * NF + 1)
                        dve.sem_inc(passed_dve, 1)

                        def h_tile(i):
                            if i == 0:
                                return first[:, bass.ds(b, 1), :].rearrange("p a c -> p (a c)")
                            return acc[:, bass.ds(b * (NT - 1) + (i - 1), 1), :].rearrange("p a c -> p (a c)")

                        def stats_of(i, n):
                            nc.vector.bn_stats(stats[0:SIZE[i], i, :], h_tile(i)).then_inc(stats_done, 1)

                        def normalise(n):
                            for i in range(NT):
                                dve.wait_ge(stats_done, b * 2 * NT + n * NT + i + 1)
                                dve.sem_inc(passed_dve, 1)
                                nc.vector.bn_aggr(mean_var[0:SIZE[i], i, :], stats[0:SIZE[i], i, :]).then_inc(aggr_done, 1)
                            dve.wait_ge(aggr_done, b * 2 * NT + n * NT + NT)
                            nc.vector.tensor_scalar(var_eps[0:T0, 0:1], mean_var[0:T0, 0, 1:2], LN_EPS, None, ALU.add)
                            nc.vector.tensor_scalar(var_eps[:, 1:NT], mean_var[:, 1:NT, 1], LN_EPS, None,
                                                    ALU.add).then_inc(eps_done, 1)
                            dve.wait_ge(rstd_done, b * 2 + n + 1)

                        def xhat_of(i, n, kind):
                            if i >= 2:
                                dve.wait_ge(unit_ready, b * NU + UNIT[(kind, i - 2)] + 1)
                            nc.vector.tensor_scalar(xhat[0:SIZE[i], i % 2, :], h_tile(i), mean_var[0:SIZE[i], i, 0:1],
                                                    rstd[0:SIZE[i], i:i + 1], ALU.subtract, ALU.mult
                                                    ).then_inc(xhat_done, 1)

                        def lower(u, dst, src, top):
                            dve.wait_ge(hi_done, b * len(HI) + HI[u] + 1)
                            nc.vector.tensor_tensor(dst, src, top, ALU.subtract).then_inc(unit_free, 1)

                        def lower_x(i):
                            u = ("xT", i)
                            cols = slice(START[i], START[i] + SIZE[i])
                            lower(u, xlo[:, :, cols],
                                  work[:, BANKS[u][0], 0:CC * 128].rearrange("p (c n) -> p c n", c=CC)[:, :, 0:SIZE[i]],
                                  xhi[:, :, cols].bitcast(F32))

                        def lower_qk(kind, p):
                            u = (kind, p)
                            k = "QK".index(kind)
                            lower(u, qk_lo[:, p % 2, k, :].rearrange("p (s n) -> p s n", s=2),
                                  work[:, BANKS[u][0]:BANKS[u][0] + 2, 0:HT],
                                  qk_hi[:, p % 2, k, :].bitcast(F32).rearrange("p (s n) -> p s n", s=2))

                        def masked(p, i):
                            u = ("S", p, i)
                            dve.wait_ge(unit_ready, b * NU + UNIT[u] + 1)
                            dve.sem_inc(passed_dve, 1)
                            for h in range(2):
                                rows = slice(0, SIZE[i])
                                at = START[-1] - START[i]
                                if i == 4:
                                    src = work[rows, 2 * h:2 * h + 2, 0:HT]
                                    dst = prob[rows, p % 2, h, P_AT[i]:P_AT[i] + TP].rearrange("p (s n) -> p s n", s=2)
                                    m = mask[rows, 0:TP].rearrange("p (s n) -> p s n", s=2)
                                else:
                                    src = work[rows, BANKS[u][h], 0:SEEN[i]]
                                    dst = prob[rows, p % 2, h, P_AT[i]:P_AT[i] + SEEN[i]]
                                    m = mask[rows, at:at + SEEN[i]]
                                nc.vector.tensor_tensor_reduce(dst, src, m, 1.0, 3.0e38, ALU.add, ALU.min,
                                                               low[rows, p % 2, i, h:h + 1]).then_inc(unit_free, 1)

                        def shares(p, i):
                            dve.wait_ge(exp_done, b * NS + S_NO[p, i, 1] + 1)
                            nc.vector.reciprocal(share[0:SIZE[i], p % 2, i, :],
                                                 total[0:SIZE[i], p % 2, i, :]).then_inc(share_done, 1)

                        def take_turned(p, j):
                            dve.wait_ge(turn_ready[1], b * NPAIR * NTURN + p * NTURN + j + 1)
                            if j >= 2:
                                dve.wait_ge(pv_done, b * NPAIR * NT + p * NT + j - 1)
                            elif p:
                                dve.wait_ge(pv_done, b * NPAIR * NT + p * NT)
                            w = 512 - (START[max(j, 1)] - T0)
                            nc.vector.tensor_copy(probT[0:SIZE[j], j % 2, 1, 0:w],
                                                  turned[1][0:SIZE[j], 0:w]).then_inc(turn_done[1], 1)

                        for i in range(NT):
                            stats_of(i, 0)
                        normalise(0)
                        xhat_of(0, 0, "xT")
                        xhat_of(1, 0, "xT")
                        for i in range(NT):
                            lower_x(i)
                            if i + 2 < NT:
                                xhat_of(i + 2, 0, "xT")
                        for i in range(NT):
                            for half in range(2):
                                u = ("V", i, half)
                                dve.wait_ge(unit_ready, b * NU + UNIT[u] + 1)
                                nc.vector.tensor_copy(v[0:SIZE[i], i, half * 512:half * 512 + 512],
                                                      work[0:SIZE[i], BANKS[u][0], :]).then_inc(unit_free, 1)
                        lower_qk("Q", 0)
                        lower_qk("K", 0)
                        for i in (4, 3, 2, 1, 0):
                            masked(0, i)
                            if i < 4:
                                shares(0, i + 1)
                        shares(0, 0)
                        for p in range(NPAIR):
                            more = p + 1 < NPAIR
                            if more:
                                lower_qk("Q", p + 1)
                                lower_qk("K", p + 1)
                            take_turned(p, 0)
                            take_turned(p, 1)
                            for j in range(NT):
                                if more:
                                    masked(p + 1, 4 - j)
                                if j + 2 < NT:
                                    take_turned(p, j + 2)
                                elif j + 2 == NT:
                                    dve.wait_ge(turn_ready[1], b * NPAIR * NTURN + (p + 1) * NTURN)
                                    if p:
                                        dve.wait_ge(y_ready, b * NPAIR + p)
                                    nc.vector.tensor_copy(probT0[:, 1, :],
                                                          turned[1][0:T0, 0:T0]).then_inc(turn_done[1], 1)
                                if more:
                                    shares(p + 1, 4 - j)

                        for i in range(NT):
                            u = ("O", i)
                            dve.wait_ge(unit_ready, b * NU + UNIT[u] + 1)
                            nc.vector.tensor_tensor(h_tile(i), work[0:SIZE[i], BANKS[u][0], 0:C], h_tile(i),
                                                    ALU.add).then_inc(unit_free, 1)
                            dve.wait_ge(unit_free, b * NF + FREED[u])
                            dve.sem_inc(passed_dve, 1)
                            stats_of(i, 1)
                        normalise(1)
                        xhat_of(0, 1, "x2T")
                        xhat_of(1, 1, "x2T")
                        for i in range(NT):
                            u = ("x2T", i)
                            dve.wait_ge(unit_ready, b * NU + UNIT[u] + 1)
                            src = work[:, BANKS[u][0], 0:CC * 128].rearrange("p (c n) -> p c n", c=CC)[:, :, 0:SIZE[i]]
                            if i == 0:
                                dst = x2T[:, :, bass.ds(b * T0 + REST, T0)]
                            else:
                                dst = x2T[:, :, bass.ds(b * TXT + (i - 1) * 128, 128)]
                            nc.vector.tensor_copy(dst, src).then_inc(unit_free, 1)
                            if i + 2 < NT:
                                xhat_of(i + 2, 1, "x2T")

        with ExitStack() as two:
            def sb(name, shape, dt=F32):
                return two.enter_context(nc.sbuf_tensor(name, shape, dt))

            WE = 2 * CC * F + FT * C
            x2hi = sb("x2hi", [128, CC, NTOK], F32R)
            x2lo = sb("x2lo", [128, CC, NTOK], F32R)
            wraw = sb("wraw", [128, WE])
            wehi = sb("wehi", [128, 2, WE], F32R)
            welo = sb("welo", [128, 2, WE], F32R)
            fhi = sb("fhi", [128, 2, FT, 512], F32R)
            flo = sb("flo", [128, 2, FT, 512], F32R)
            silu = sb("silu", [128, 2, 512])
            fuse = sb("fuse", [128, 2, 512])
            mixed = sb("mixed", [128, 2, C])
            wr = sb("wr", [128, CC, E])
            logitT = sb("logitT", [E, NTOK])
            logit = sb("logit", [128, ND, E])
            pr = sb("pr", [128, ND, E])
            eq = sb("eq", [128, ND, E])
            run = sb("run", [128, ND, E])
            one_hot = sb("one_hot", [128, 2, ND, E])
            gatew = sb("gatew", [128, ND, E])
            wcol = sb("wcol", [128, 2, ND])
            r1 = sb("r1", [128, 8, ND])

            wr_in, moved, raw_in = sem("wr_in"), sem("moved"), sem("raw_in")
            x2_hi, x2_lo = sem("x2_hi"), sem("x2_lo")
            lt_ready, lt_done, l_ready, l_done = (sem(n) for n in ("lt_ready", "lt_done", "l_ready", "l_done"))
            l_zero = sem("l_zero")
            step = sem("step")
            exp_asked, exp_given = sem("exp_asked"), sem("exp_given")
            we_hi, we_lo = sem("we_hi"), sem("we_lo")
            gu_ready, silu_done, fuse_done, fhi_done, flo_done = (
                sem(n) for n in ("gu_ready", "silu_done", "fuse_done", "fhi_done", "flo_done"))
            down_ready, down_done = sem("down_ready"), sem("down_done")
            wcol_done, stored = sem("wcol_done"), sem("stored")
            NC = len(CHUNKS)
            GU_AHEAD, DOWN_AHEAD = 1, 4
            NG = NC * FT
            SPLITS = [(c, lo, hi) for lo, hi in CHUNKS for c in range(CC)]
            dbanks = [turned[0], turned[1], y_text, y_first]

            def acc_of(k):
                if k < B * (NT - 1):
                    return acc[:, k, :]
                return mixed[0:DOWN[k][1], k - B * (NT - 1), :]

            with nc.Block() as block:
                def part(buf, s, what, *at):
                    if what == "down":
                        f = at[0]
                        o = 2 * CC * F + f * C
                        return buf[:, s, o:o + C]
                    c, f = at
                    o = (CC * F if what == "up" else 0) + c * F + f * 128
                    return buf[:, s, o:o + 128]

                @block.sync
                def _(sp):
                    sp.dma_start(wr[:, :, :], w_router.rearrange("(c p) e -> p c e", p=128)).then_inc(wr_in, 16)
                    for b in range(B):
                        dst = mixed[T0 * b:T0 * (b + 1), 0, :] if b < 3 else mixed[0:T0, 1, :]
                        sp.dma_start(dst, first[:, b, :]).then_inc(moved, 16)

                    def load(e):
                        sp.dma_start(wraw[:, 0:CC * F].rearrange("p (c f) -> p c f", c=CC),
                                     w_gate[e].rearrange("(c p) f -> p c f", p=128)).then_inc(raw_in, 16)
                        sp.dma_start(wraw[:, CC * F:2 * CC * F].rearrange("p (c f) -> p c f", c=CC),
                                     w_up[e].rearrange("(c p) f -> p c f", p=128)).then_inc(raw_in, 16)
                        sp.dma_start(wraw[:, 2 * CC * F:].rearrange("p (f d) -> p f d", f=FT),
                                     w_down[e].rearrange("(f p) d -> p f d", p=128)).then_inc(raw_in, 16)

                    load(0)
                    with sp.Fori(0, E - 1) as e:
                        sp.wait_ge(we_lo, e + 1)
                        load(e + 1)
                    last = (E - 1) * ND
                    order = [k for c in range(NC) for k in chunk_tiles(c)]
                    for n, k in enumerate(order):
                        sp.wait_ge(down_done, DOWN_AHEAD + last + n + 1)
                        if k < B * (NT - 1):
                            b, i = k // (NT - 1), k % (NT - 1)
                            sp.dma_start(out[b, T0 + 128 * i:T0 + 128 * i + 128, :], acc[:, k, :]).then_inc(stored, 16)
                        elif k == B * (NT - 1):
                            for b in range(3):
                                sp.dma_start(out[b, 0:T0, :], mixed[T0 * b:T0 * (b + 1), 0, :]).then_inc(stored, 16)
                        else:
                            sp.dma_start(out[3, 0:T0, :], mixed[0:T0, 1, :]).then_inc(stored, 16)
                    sp.wait_ge(stored, 16 * (B * (NT - 1) + B))

                def tiles_before(c):
                    return sum(len(chunk_tiles(k)) for k in range(c))

                def experts(eng, body):
                    with eng.Fori(0, E // 2 - 1) as pair:
                        for s in range(2):
                            body(pair * 2 + s, s, False)
                    for s in range(2):
                        body(E - 2 + s, s, s == 1)

                STEPS = [(c + 1, c) for c in range(NC - 1)] + [(NC, NC - 1)]

                @block.tensor
                def _(pe):
                    pe.sem_inc(down_ready, 1)
                    pe.wait_ge(wr_in, 16)
                    for n, (lo, hi) in enumerate(CHUNKS):
                        if n >= 2:
                            pe.wait_ge(lt_done, n - 1)
                        for c in range(CC):
                            mm = nc.tensor.matmul(dbanks[2 + n % 2][0:E, 0:hi - lo], wr[:, c, :], x2T[:, c, lo:hi],
                                                  start=(c == 0), stop=(c == CC - 1))
                        mm.then_inc(lt_ready, 1)
                    pe.wait_ge(lt_done, NC)
                    for k, (at, rows) in enumerate(DOWN):
                        mm = nc.tensor.transpose(turned[0][0:rows, k * E:k * E + E], logitT[:, at:at + rows],
                                                 ident[0:E, 0:E])
                    mm.then_inc(l_ready, 1)

                    def gate_up(e, s, c, f):
                        lo, hi = CHUNKS[c]
                        bank = 2 * ((c * FT + f) % 2)
                        if not (isinstance(e, int) and e == 0 and c * FT + f == 0):
                            pe.wait_ge(fuse_done, GU_AHEAD + e * NG + c * FT + f - 1)
                        for w, what in enumerate(("gate", "up")):
                            dst = work[:, bank + w, 0:hi - lo]
                            for k in range(CC):
                                wh, wl = part(wehi, s, what, k, f), part(welo, s, what, k, f)
                                xh, xl = x2hi[:, k, lo:hi], x2lo[:, k, lo:hi]
                                nc.tensor.matmul(dst, wh, xh, start=(k == 0), stop=False)
                                nc.tensor.matmul(dst, wh, xl, start=False, stop=False)
                                mm = nc.tensor.matmul(dst, wl, xh, start=False, stop=(k == CC - 1))
                        mm.then_inc(gu_ready, 1)

                    def down(e, s, c, t):
                        at, rows = DOWN[chunk_tiles(c)[t]]
                        off = at - CHUNKS[c][0]
                        n = tiles_before(c) + t
                        if t == 0:
                            pe.wait_ge(flo_done, e * NG + (c + 1) * FT)
                        pe.wait_ge(down_done, DOWN_AHEAD + e * ND + n - 3)
                        dst = dbanks[(s * ND + n) % 4][0:rows, 0:C]
                        for f in range(FT):
                            fh, fl = (x[:, (s * NC + c) % 2, f, off:off + rows] for x in (fhi, flo))
                            dh, dl = part(wehi, s, "down", f), part(welo, s, "down", f)
                            nc.tensor.matmul(dst, fh, dh, start=(f == 0), stop=False)
                            nc.tensor.matmul(dst, fh, dl, start=False, stop=False)
                            mm = nc.tensor.matmul(dst, fl, dh, start=False, stop=(f == FT - 1))
                        mm.then_inc(down_ready, 1)

                    def body(e, s, last):
                        for c, before in STEPS:
                            tiles = len(chunk_tiles(before))
                            if c == NC and last:
                                for t in range(tiles):
                                    down(e, s, before, t)
                                continue
                            if c == NC:
                                pe.wait_ge(we_lo, e + 2)
                            nxt = (e + 1, 1 - s, 0) if c == NC else (e, s, c)
                            for f in range(FT):
                                gate_up(*nxt, f)
                                if f:
                                    down(e, s, before, f - 1)
                            for t in range(FT - 1, tiles):
                                down(e, s, before, t)

                    pe.wait_ge(x2_lo, len(SPLITS))
                    pe.wait_ge(we_lo, 1)
                    pe.wait_ge(l_done, 3)
                    for f in range(FT):
                        gate_up(0, 0, 0, f)
                    experts(pe, body)

                @block.scalar
                def _(act):
                    for n, (c, lo, hi) in enumerate(SPLITS):
                        nc.scalar.activation(x2hi[:, c, lo:hi], x2T[:, c, lo:hi], ACT.Copy).then_inc(x2_hi, 1)

                    def weights_upper(e, s):
                        act.wait_ge(raw_in, e * 48 + 48)
                        nc.scalar.activation(wehi[:, s, :], wraw[:, :], ACT.Copy).then_inc(we_hi, 1)

                    weights_upper(0, 0)
                    act.wait_ge(exp_asked, 1)
                    nc.scalar.activation(pr[:, :, :], pr[:, :, :], ACT.Exp).then_inc(exp_given, 1)
                    act.wait_ge(exp_asked, 2)
                    nc.scalar.activation(r1[:, 3, :], r1[:, 2, :], ACT.Exp).then_inc(exp_given, 1)

                    def gate(e, s, c, f):
                        n = c * FT + f
                        w = CHUNKS[c][1] - CHUNKS[c][0]
                        act.wait_ge(gu_ready, e * NG + n + 1)
                        nc.scalar.activation(silu[:, n % 2, 0:w], work[:, 2 * (n % 2), 0:w],
                                             ACT.Silu).then_inc(silu_done, 1)

                    def upper(e, s, c, f):
                        n = c * FT + f
                        w = CHUNKS[c][1] - CHUNKS[c][0]
                        act.wait_ge(fuse_done, GU_AHEAD + e * NG + n + 1)
                        nc.scalar.activation(fhi[:, (s * NC + c) % 2, f, 0:w], fuse[:, n % 2, 0:w],
                                             ACT.Copy).then_inc(fhi_done, 1)

                    def body(e, s, last):
                        for c, before in STEPS:
                            if c == NC and last:
                                upper(e, s, before, FT - 1)
                                continue
                            nxt = (e + 1, 1 - s, 0) if c == NC else (e, s, c)
                            for f in range(FT):
                                gate(*nxt, f)
                                if f == 0:
                                    upper(e, s, before, FT - 1)
                                    act.wait_ge(down_ready, 1 + e * ND + tiles_before(c - 1))
                                else:
                                    upper(*nxt, f - 1)
                            if c == 2 and not last:
                                weights_upper(e + 1, 1 - s)

                    for f in range(FT):
                        gate(0, 0, 0, f)
                        if f:
                            upper(0, 0, 0, f - 1)
                    experts(act, body)

                @block.vector
                def _(dve):
                    nc.vector.memset(logit[:, :, :], 0.0).then_inc(l_zero, 1)
                    dve.sem_inc(fuse_done, GU_AHEAD)
                    dve.sem_inc(down_done, DOWN_AHEAD)

                    def take_logits(n):
                        lo, hi = CHUNKS[n]
                        dve.wait_ge(lt_ready, n + 1)
                        nc.vector.tensor_copy(logitT[:, lo:hi], dbanks[2 + n % 2][0:E, 0:hi - lo]).then_inc(lt_done, 1)

                    for n, (c, lo, hi) in enumerate(SPLITS):
                        dve.wait_ge(x2_hi, n + 1)
                        nc.vector.tensor_tensor(x2lo[:, c, lo:hi], x2T[:, c, lo:hi], x2hi[:, c, lo:hi].bitcast(F32),
                                                ALU.subtract).then_inc(x2_lo, 1)
                        if n % 2:
                            take_logits(n // 2)

                    def weights_lower(e, s):
                        dve.wait_ge(we_hi, e + 1)
                        nc.vector.tensor_tensor(welo[:, s, :], wraw[:, :], wehi[:, s, :].bitcast(F32),
                                                ALU.subtract).then_inc(we_lo, 1)

                    dve.wait_ge(l_ready, 1)
                    dve.wait_ge(l_zero, 1)
                    full = B * (NT - 1)
                    bank = turned[0][:, 0:ND * E].rearrange("p (k e) -> p k e", e=E)
                    for rows, a, b in ((128, 0, full), (X_ROWS, full, full + 1), (T0, full + 1, ND)):
                        nc.vector.tensor_copy(logit[0:rows, a:b, :], bank[0:rows, a:b, :]).then_inc(l_done, 1)
                    dve.wait_ge(l_done, 3)
                    weights_lower(0, 0)

                    links = [0]

                    def link(ins):
                        ins.then_inc(step, 1)
                        links[0] += 1
                        dve.wait_ge(step, links[0])

                    def spread(a):
                        return a.unsqueeze(2).to_broadcast([128, ND, E])

                    link(nc.vector.tensor_reduce(r1[:, 0, :], logit[:, :, :], AX.X, ALU.max))
                    nc.vector.tensor_tensor(pr[:, :, :], logit[:, :, :], spread(r1[:, 0, :]),
                                            ALU.subtract).then_inc(exp_asked, 1)
                    dve.wait_ge(exp_given, 1)
                    link(nc.vector.tensor_reduce(r1[:, 7, :], pr[:, :, :], AX.X, ALU.add))
                    link(nc.vector.reciprocal(r1[:, 0, :], r1[:, 7, :]))
                    link(nc.vector.tensor_tensor(pr[:, :, :], pr[:, :, :], spread(r1[:, 0, :]), ALU.mult))

                    def highest(n, to):
                        link(nc.vector.tensor_reduce(r1[:, to, :], pr[:, :, :], AX.X, ALU.max))
                        link(nc.vector.tensor_tensor(eq[:, :, :], pr[:, :, :], spread(r1[:, to, :]), ALU.is_equal))
                        link(nc.vector.tensor_copy(run[:, :, 0], eq[:, :, 0]))
                        for k in range(1, E):
                            link(nc.vector.tensor_tensor(run[:, :, k], run[:, :, k - 1], eq[:, :, k], ALU.add))
                        link(nc.vector.scalar_tensor_tensor(out=one_hot[:, n, :, :], in0=run[:, :, :], scalar=1.0,
                                                            in1=eq[:, :, :], op0=ALU.is_equal, op1=ALU.mult))

                    highest(0, 1)
                    link(nc.vector.scalar_tensor_tensor(out=pr[:, :, :], in0=one_hot[:, 0, :, :], scalar=-2.0,
                                                        in1=pr[:, :, :], op0=ALU.mult, op1=ALU.add))
                    highest(1, 4)
                    nc.vector.tensor_tensor(r1[:, 2, :], r1[:, 4, :], r1[:, 1, :], ALU.subtract).then_inc(exp_asked, 1)
                    dve.wait_ge(exp_given, 2)
                    link(nc.vector.tensor_scalar(r1[:, 5, :], r1[:, 3, :], 1.0, None, ALU.add))
                    link(nc.vector.reciprocal(r1[:, 6, :], r1[:, 5, :]))
                    link(nc.vector.tensor_tensor(r1[:, 7, :], r1[:, 3, :], r1[:, 6, :], ALU.mult))
                    link(nc.vector.tensor_tensor(gatew[:, :, :], one_hot[:, 0, :, :], spread(r1[:, 6, :]), ALU.mult))
                    link(nc.vector.tensor_tensor(run[:, :, :], one_hot[:, 1, :, :], spread(r1[:, 7, :]), ALU.mult))
                    link(nc.vector.tensor_tensor(gatew[:, :, :], gatew[:, :, :], run[:, :, :], ALU.add))
                    dve.wait_ge(moved, 16 * B)

                    def fused(e, s, c, f):
                        n = c * FT + f
                        w = CHUNKS[c][1] - CHUNKS[c][0]
                        if not (isinstance(e, int) and e == 0 and n < 2):
                            dve.wait_ge(flo_done, e * NG + n - 1)
                        dve.wait_ge(silu_done, e * NG + n + 1)
                        nc.vector.tensor_tensor(fuse[:, n % 2, 0:w], work[:, 2 * (n % 2) + 1, 0:w],
                                                silu[:, n % 2, 0:w], ALU.mult).then_inc(fuse_done, 1)

                    def lower(e, s, c, f):
                        n = c * FT + f
                        w = CHUNKS[c][1] - CHUNKS[c][0]
                        fs = (s * NC + c) % 2
                        dve.wait_ge(fhi_done, e * NG + n + 1)
                        nc.vector.tensor_tensor(flo[:, fs, f, 0:w], fuse[:, n % 2, 0:w],
                                                fhi[:, fs, f, 0:w].bitcast(F32), ALU.subtract).then_inc(flo_done, 1)

                    def add(e, s, c, t):
                        k = chunk_tiles(c)[t]
                        rows = DOWN[k][1]
                        n = tiles_before(c) + t
                        dve.wait_ge(down_ready, 1 + e * ND + n + 1)
                        dst = acc_of(k)
                        nc.vector.scalar_tensor_tensor(out=dst, in0=dbanks[(s * ND + n) % 4][0:rows, 0:C],
                                                       scalar=wcol[0:rows, s, k:k + 1], in1=dst,
                                                       op0=ALU.mult, op1=ALU.add).then_inc(down_done, 1)

                    def body(e, s, last):
                        nc.vector.tensor_copy(wcol[:, s, :], gatew[:, :, bass.ds(e, 1)].rearrange("p k a -> p (k a)")
                                              ).then_inc(wcol_done, 1)
                        dve.wait_ge(wcol_done, e + 1)
                        for c, before in STEPS:
                            tiles = len(chunk_tiles(before))
                            if c == NC and last:
                                lower(e, s, before, FT - 1)
                                for t in range(tiles):
                                    add(e, s, before, t)
                                continue
                            nxt = (e + 1, 1 - s, 0) if c == NC else (e, s, c)
                            for f in range(FT):
                                fused(*nxt, f)
                                if f == 0:
                                    lower(e, s, before, FT - 1)
                                else:
                                    lower(*nxt, f - 1)
                                if f >= 2:
                                    add(e, s, before, f - 2)
                            for t in range(FT - 2, tiles):
                                add(e, s, before, t)
                            if c == 2 and not last:
                                weights_lower(e + 1, 1 - s)

                    for f in range(FT):
                        fused(0, 0, 0, f)
                        if f:
                            lower(0, 0, 0, f - 1)
                    experts(dve, body)
    return nc


_INS = ["x", "txt", "L0_tok_W", "L0_tok_b", "L0_tok_cls_token", "L0_tok_pos_emb", "L0_attn_w_q", "L0_attn_w_k",
        "L0_attn_w_v", "L0_attn_w_o", "L0_ffn_kernel_router_DE", "L0_ffn_kernel_gating_EDF",
        "L0_ffn_kernel_up_EDF", "L0_ffn_kernel_down_EFD"]


def kernel(**inputs):
    import numpy as np
    import concourse.bacc as bacc
    from concourse.bass_utils import run_bass_kernel_spmd

    nc = bacc.Bacc("TRN2", target_bir_lowering=False, num_devices=1)
    arrays, args = {}, []
    for name in _INS:
        a = np.ascontiguousarray(inputs[name])
        arrays[f"in_{name}"] = a
        args.append(nc.dram_tensor(f"in_{name}", a.shape, mybir.dt.from_np(a.dtype), kind="ExternalInput").ap())
    args.append(nc.dram_tensor("out", (B, T, C), F32, kind="ExternalOutput").ap())
    fusion_block_kernel(nc, *args)
    r = run_bass_kernel_spmd(nc, [arrays], core_ids=[0])
    return r.results[0]["out"]
```

```python
from contextlib import ExitStack

import concourse.bass as bass
from concourse import mybir

F32 = mybir.dt.float32
F32R = mybir.dt.float32r
ALU = mybir.AluOpType
ACT = mybir.ActivationFunctionType
AX = mybir.AxisListType

B, CH, IMG, P = 4, 3, 96, 16
C = 256
CC = C // 128
G = IMG // P
NP = G * G
TXT = 512
T0 = NP + 1
NT = 1 + TXT // 128
T = T0 + TXT
TP = 552
HT = TP // 2
H, D = 16, 64
HD = H * D
NPAIR = H // 2
E, F = 8, 512
FT = F // 128
LN_EPS = 1e-5
Q_SCALE = -1.0 / D ** 0.5
MASKED = 1e30

SIZE = [T0] + [128] * (NT - 1)
START = [0] + [T0 + 128 * i for i in range(NT - 1)]
SEEN = [START[i] + SIZE[i] for i in range(NT)]
P_AT = [sum(SEEN[:i]) for i in range(NT)]
P_LEN = P_AT[-1] + TP

NTOK = B * T
REST = B * TXT
CHUNKS = [(0, 512), (512, 1024), (1024, 1536), (1536, 1920), (1920, NTOK)]
X_ROWS = 3 * T0
DOWN = [(128 * k, 128) for k in range(B * (NT - 1))] + [(REST, X_ROWS), (REST + X_ROWS, T0)]
ND = len(DOWN)


def chunk_tiles(c):
    lo, hi = CHUNKS[c]
    return [k for k, (at, _) in enumerate(DOWN) if lo <= at < hi]


NTURN = NT
NS = NT * 2
DOWNWARD = tuple(reversed(range(NT)))
BY_DVE = (2, 1)
BY_POOL = [(i, h) for i in DOWNWARD for h in range(2) if (i, h) != BY_DVE]
TURNS = [range(0, 1), range(1, 3), range(3, 5)]
STARTED = [("xT", g) for g in range(len(TURNS))] + [("Q", 0), ("K", 0)] + [("S", 0, i) for i in DOWNWARD]
EARLY = 4
VALUES = [("V", i, half) for i in range(NT) for half in range(2)]
FIRST = STARTED[:len(TURNS) + 2] + [u for k, i in enumerate(DOWNWARD) for u in VALUES[2 * k:2 * k + 2] + [("S", 0, i)]]
ENDED = [("x2T", g) for g in range(len(TURNS))]


def turned_tokens(g):
    return START[TURNS[g][0]], START[TURNS[g][-1]] + SIZE[TURNS[g][-1]]


class Frame:

    def __init__(self, units, ready, free, hi, first_bank=0, held={}, values_apart=False):
        self.units, self.ready0, self.free0, self.hi0 = units, ready, free, hi
        self.banks, self.number, self.before, self.freed, self.hi = {}, {}, {}, {}, {}
        turn, count = first_bank, 0
        last = dict(held)
        for n, u in enumerate(units):
            if u[0] == "S":
                self.banks[u] = [0, 1, 2, 3] if u[2] == NT - 1 else [0, 1] if u[2] % 2 else [2, 3]
            elif u[0] in "QK":
                self.banks[u] = [0, 1] if u[0] == "Q" else [2, 3]
            elif values_apart and u[0] == "V":
                self.banks[u] = [4 + VALUES.index(u) % 4]
            else:
                self.banks[u] = [turn % 4]
                turn += 1
            if u[0] in ("xT", "Q", "K"):
                self.hi[u] = len(self.hi) + 1
            self.number[u] = n + 1
            self.before[u] = max([last.get(b, -free) for b in self.banks[u]])
            count += 2 if u[0] == "S" else 1
            self.freed[u] = count
            for b in self.banks[u]:
                last[b] = count - (len(self.banks[u]) == 4 and b < 2)
        self.n_ready, self.n_free, self.n_hi = len(units), count, len(self.hi)
        self.left = {b: n - count for b, n in last.items()}

    def is_ready(self, u):
        return self.ready0 + self.number[u]

    def is_free(self, u):
        return self.free0 + self.freed[u]

    def is_hi(self, u):
        return self.hi0 + self.hi[u]


def batch_units(last):
    units = []
    for p in range(1, NPAIR):
        units += [("Q", p), ("K", p)] + [("S", p, i) for i in DOWNWARD]
    if not last:
        units += STARTED + VALUES[:EARLY]
    units += [("O", i) for i in range(NT)]
    return units + ([] if last else VALUES[EARLY:]) + ENDED


def fusion_block_kernel(nc, x, txt, tok_w, tok_b, cls_token, pos_emb, w_q, w_k, w_v, w_o,
                        w_router, w_gate, w_up, w_down, out):
    ctx = ExitStack()
    with ctx:
        def sem(name):
            return ctx.enter_context(nc.semaphore(name))

        def keep(name, shape, dt=F32):
            return ctx.enter_context(nc.sbuf_tensor(name, shape, dt))

        acc = keep("acc", [128, B * (NT - 1), C])
        first = keep("first", [T0, B, C])
        x2T = keep("x2T", [128, CC, NTOK])
        ident = keep("ident", [128, 128])
        work = ctx.enter_context(nc.psum_tensor("work", [128, 4, 512], F32))
        turned = [ctx.enter_context(nc.psum_tensor(f"turned{h}", [128, 512], F32)) for h in range(2)]
        y_text = ctx.enter_context(nc.psum_tensor("y_text", [128, 512], F32))
        y_first = ctx.enter_context(nc.psum_tensor("y_first", [128, 512], F32))
        banks = [work[:, k, :] for k in range(4)] + [turned[0], turned[1], y_text, y_first]

        with ExitStack() as one:
            def sb(name, shape, dt=F32):
                return one.enter_context(nc.sbuf_tensor(name, shape, dt))

            whi = sb("whi", [128, 3, CC, HD], F32R)
            wlo = sb("wlo", [128, 3, CC, HD], F32R)
            wo = sb("wo", [128, NPAIR, C])
            xhi = sb("xhi", [128, CC, TP], F32R)
            xlo = sb("xlo", [128, CC, TP], F32R)
            v = sb("v", [128, NT, HD])
            prob = sb("prob", [128, 2, 2, P_LEN])
            probT = sb("probT", [128, 2, 2, 512])
            probT0 = sb("probT0", [T0, 2, T0])
            yT = sb("yT", [128, NPAIR, TP])
            qk_hi = sb("qk_hi", [128, 2, 2, TP], F32R)
            qk_lo = sb("qk_lo", [128, 2, 2, TP], F32R)
            xhat = sb("xhat", [128, NT, C])
            mask = sb("mask", [128, TP + START[-1]])
            low = sb("low", [128, 2, NT, 2])
            total = sb("total", [128, 2, NT, 2])
            share = sb("share", [128, 2, NT, 2])
            stats = sb("stats", [128, NT, 6])
            mean_var = sb("mean_var", [128, NT, 2])
            var_eps = sb("var_eps", [128, NT])
            rstd = sb("rstd", [128, NT])
            minus_half = sb("minus_half", [128, NT])
            extra = sb("extra", [T0, 2, C])
            pflat = prob[:, :, :, :].rearrange("p a h n -> p (a h n)")
            raw = [pflat[:, 0:8 * C].rearrange("p (r c) -> p r c", r=8),
                   pflat[:, 8 * C:16 * C].rearrange("p (r c) -> p r c", r=8),
                   yT[:, :, :].rearrange("p a n -> p (a n)")[:, 0:8 * C].rearrange("p (r c) -> p r c", r=8)]
            KP, DX = CH * P, P // 2
            tokw = v[0:2 * KP, :, :].rearrange("p a n -> p (a n)")[:, 0:DX * C].rearrange("p (d e) -> p d e", d=DX)
            COLS = 64 + T0
            px = x2T[0:2 * KP, :, :].rearrange("p a n -> p (a n)")[:, 0:2 * COLS * P].rearrange(
                "p (g s d) -> p g s d", g=2, d=P)

            w_in = [sem(f"w_in{m}") for m in range(3)]
            px_in = [sem(f"px_in{g}") for g in range(2)]
            px_shifted = [sem(f"px_shifted{g}") for g in range(2)]
            wo_in, tokw_in, extra_in, txt0_in, txt_in = (sem(n) for n in ("wo_in", "tokw_in", "extra_in", "txt0_in", "txt_in"))
            ident_made, mask_made, half_made = sem("ident_made"), sem("mask_made"), sem("half_made")
            px_zero = sem("px_zero")
            pads = sem("pads")
            w_turned, w_hi, w_lo = sem("w_turned"), sem("w_hi"), sem("w_lo")
            patch_ready, patch_done, extra_done = sem("patch_ready"), sem("patch_done"), sem("extra_done")
            unit_ready, unit_free = sem("unit_ready"), sem("unit_free")
            hi_done = sem("hi_done")
            stats_done, aggr_done, eps_done, rstd_done, xhat_done = (
                sem(n) for n in ("stats_done", "aggr_done", "eps_done", "rstd_done", "xhat_done"))
            h2_done = sem("h2_done")
            exp_done, share_done, norm_done, norm_dve_done = (
                sem(n) for n in ("exp_done", "share_done", "norm_done", "norm_dve_done"))
            turn_ready = [sem(f"turn_ready{h}") for h in range(2)]
            turn_done = [sem(f"turn_done{h}") for h in range(2)]
            pv_done, y_ready, y_done = sem("pv_done"), sem("y_ready"), sem("y_done")
            passed_dve, passed_pe = sem("passed_dve"), sem("passed_pe")
            first0_ready, first0_done = sem("first0_ready"), sem("first0_done")

            start = Frame(FIRST, 0, 1, 0, values_apart=True)
            FIRST_BANK = (4 - len([u for u in batch_units(False) if u[0] not in "QKS"])) % 4
            one_batch = Frame(batch_units(False), 0, 0, 0, FIRST_BANK)
            held = {b: max(start.left[b], one_batch.left[b]) for b in range(4)}

            def frame_of(b, last):
                return Frame(batch_units(last), start.n_ready + b * one_batch.n_ready,
                             1 + start.n_free + b * one_batch.n_free, start.n_hi + b * one_batch.n_hi,
                             FIRST_BANK, held)

            def batches(eng, begin, body):
                begin(start)
                with eng.Fori(0, B - 1) as b:
                    body(b, frame_of(b, False), False)
                body(B - 1, frame_of(B - 1, True), True)

            def norm_no(b, which, last=False):
                return 2 * b + (1 if which == 0 or last else 2)

            with nc.Block() as block:
                W_UNITS = [(m, c, half) for m in range(3) for c in range(CC) for half in range(2)]

                @block.sync
                def _(sp):
                    def load_txt(b):
                        sp.dma_start(acc[:, b * (NT - 1):(b + 1) * (NT - 1), :], txt[b].rearrange(
                            "(r p) c -> p r c", p=128)).then_inc(txt_in if b else txt0_in, 16)

                    def load_images(g):
                        for side in range(2):
                            for ch in range(CH):
                                sp.dma_start(
                                    px[ch * P:(ch + 1) * P, g, 64 * side + 1:64 * side + T0, :].rearrange(
                                        "y (r q) d -> y r (q d)", r=G),
                                    x[2 * g + side, ch].rearrange("(r y) w -> y r w", y=P)).then_inc(px_in[g], 16)

                    def shift_images(g):
                        sp.wait_ge(px_in[g], 16 * 2 * CH)
                        flat = px[:, g, :, :].rearrange("k s d -> k (s d)")
                        sp.dma_start(flat[KP:2 * KP, 0:COLS * P - DX], flat[0:KP, DX:COLS * P]).then_inc(px_shifted[g], 16)

                    def load_weights(m, w):
                        sp.dma_start(raw[m], w.rearrange("h d c -> (h d) c").rearrange(
                            "(r p) c -> p r c", p=128)).then_inc(w_in[m], 16)

                    load_weights(0, w_q)
                    for half in range(2):
                        for ch in range(CH):
                            row = half * KP + ch * P
                            sp.dma_start(tokw[row:row + P], tok_w.rearrange("(y x c) e -> c y x e", y=P, c=CH)[
                                ch][:, half * DX:half * DX + DX, :]).then_inc(tokw_in, 16)
                    sp.wait_ge(px_zero, 2)
                    load_images(0)
                    load_txt(0)
                    sp.dma_start(extra[:, 0, :], pos_emb).then_inc(extra_in, 16)
                    sp.dma_start(extra[0:1, 1, :], cls_token.rearrange("a b e -> (a b) e")).then_inc(extra_in, 16)
                    sp.dma_start(extra[1:T0, 1, :], tok_b.rearrange("(a e) -> a e", a=1).to_broadcast([NP, C])
                                 ).then_inc(extra_in, 16)
                    shift_images(0)
                    load_weights(1, w_k)
                    load_images(1)
                    load_weights(2, w_v)
                    shift_images(1)
                    for b in range(1, B):
                        load_txt(b)
                    sp.dma_start(wo[:, :, :], w_o.rearrange("(r p) c -> p r c", p=128)).then_inc(wo_in, 16)

                @block.gpsimd
                def _(pool):
                    nc.gpsimd.memset(ident[:, :], 1.0).then_inc(ident_made, 1)
                    pool.wait_ge(ident_made, 1)
                    nc.gpsimd.affine_select(out=ident[:, :], in_=ident[:, :], pattern=[[-1, 128]],
                                            compare_op=ALU.is_equal, fill=0.0, base=0,
                                            channel_multiplier=1).then_inc(ident_made, 1)
                    nc.gpsimd.memset(minus_half[:, :], -0.5).then_inc(half_made, 1)
                    nc.gpsimd.memset(mask[:, :], 0.0).then_inc(mask_made, 1)
                    pool.wait_ge(mask_made, 1)
                    nc.gpsimd.affine_select(out=mask[:, :], in_=mask[:, :], pattern=[[-1, TP + START[-1]]],
                                            compare_op=ALU.is_ge, fill=MASKED, base=START[-1],
                                            channel_multiplier=1).then_inc(mask_made, 1)
                    pool.wait_ge(half_made, 1)

                    def rstd_of_all(n):
                        pool.wait_ge(eps_done, n + 1)
                        nc.gpsimd.tensor_tensor(rstd[:, :], var_eps[:, :], minus_half[:, :],
                                                ALU.pow).then_inc(rstd_done, 1)

                    def norm(b, p):
                        for k, i in enumerate(DOWNWARD):
                            pool.wait_ge(share_done, (b * NPAIR + p) * NT + k + 1)
                            for h in [h for h in range(2) if (i, h) in BY_POOL]:
                                rows = prob[0:SIZE[i], p % 2, h, P_AT[i]:P_AT[i] + SEEN[i]]
                                nc.gpsimd.tensor_tensor(
                                    rows, rows, share[0:SIZE[i], p % 2, i, h:h + 1].to_broadcast(
                                        [SIZE[i], SEEN[i]]), ALU.mult).then_inc(norm_done, 1)

                    def begin(fr):
                        rstd_of_all(0)
                        norm(0, 0)

                    def body(b, fr, last):
                        for p in range(NPAIR):
                            if p + 1 < NPAIR or not last:
                                norm(b, p + 1)
                            if p == NPAIR - 3 and not last:
                                rstd_of_all(norm_no(b, 0))
                        rstd_of_all(norm_no(b, 1, last))

                    batches(pool, begin, body)

                @block.tensor
                def _(pe):
                    def patches(g):
                        pe.wait_ge(px_shifted[g], 16)
                        for d in range(DX):
                            mm = nc.tensor.matmul(turned[g][0:COLS, 0:C], px[:, g, :, d], tokw[:, d, :],
                                                  start=(d == 0), stop=(d == DX - 1))
                        mm.then_inc(patch_ready, 1)

                    def turn_weights(which):
                        for n, (m, c, half) in enumerate(W_UNITS):
                            if m != which:
                                continue
                            if c == 0 and half == 0:
                                pe.wait_ge(w_in[m], 16)
                            if n >= 4:
                                pe.wait_ge(w_lo, n - 3)
                            for r in range(4):
                                mm = nc.tensor.transpose(work[:, n % 4, r * 128:(r + 1) * 128],
                                                         raw[m][:, 4 * half + r, c * 128:(c + 1) * 128], ident[:, :])
                            mm.then_inc(w_turned, 1)

                    pe.wait_ge(ident_made, 2)
                    turn_weights(0)
                    pe.wait_ge(tokw_in, 16 * 2 * CH)
                    patches(0)
                    turn_weights(1)
                    turn_weights(2)
                    pe.wait_ge(pads, 2)
                    pe.sem_inc(pv_done, 1)

                    def claim(fr, u, after=None):
                        n = max(fr.before[u], fr.freed[after]) if after else fr.before[u]
                        if not (isinstance(fr.free0, int) and fr.free0 + n <= 0):
                            pe.wait_ge(unit_free, fr.free0 + n)

                    def three(dst, a, m, first_, last_):
                        nc.tensor.matmul(dst, a[0], m[0], start=first_, stop=False)
                        nc.tensor.matmul(dst, a[0], m[1], start=False, stop=False)
                        return nc.tensor.matmul(dst, a[1], m[0], start=False, stop=last_)

                    def turn_x(fr, kind, n, groups=range(len(TURNS))):
                        for g in groups:
                            u, tiles = (kind, g), TURNS[g]
                            claim(fr, u)
                            for i in tiles:
                                pe.wait_ge(xhat_done, n * NT + i + 1)
                                if i == 0:
                                    pe.sem_inc(passed_pe, 1)
                                for c in range(CC):
                                    at = c * 256 + (i - tiles[0]) * 128
                                    mm = nc.tensor.transpose(work[:, fr.banks[u][0], at:at + SIZE[i]],
                                                             xhat[0:SIZE[i], i, c * 128:(c + 1) * 128],
                                                             ident[0:SIZE[i], 0:SIZE[i]])
                            mm.then_inc(unit_ready, 1)

                    def values(fr, units):
                        for u in units:
                            i, half = u[1:]
                            claim(fr, u, ("xT", next(g for g, tiles in enumerate(TURNS) if i in tiles)))
                            cols = slice(START[i], START[i] + SIZE[i])
                            n = slice(half * 512, half * 512 + 512)
                            for c in range(CC):
                                mm = three(banks[fr.banks[u][0]][0:SIZE[i], :], (xhi[:, c, cols], xlo[:, c, cols]),
                                           (whi[:, 2, c, n], wlo[:, 2, c, n]), c == 0, c == CC - 1)
                            mm.then_inc(unit_ready, 1)

                    def project(fr, kind, p):
                        u = (kind, p)
                        m = "QK".index(kind)
                        claim(fr, u, ("xT", len(TURNS) - 1) if p == 0 else None)
                        rows = slice(p * 128, p * 128 + 128)
                        for s in range(2):
                            n = slice(s * HT, s * HT + HT)
                            for c in range(CC):
                                mm = three(work[:, fr.banks[u][s], 0:HT], (whi[:, m, c, rows], wlo[:, m, c, rows]),
                                           (xhi[:, c, n], xlo[:, c, n]), c == 0, c == CC - 1)
                        mm.then_inc(unit_ready, 1)

                    def scores(fr, p, i):
                        u = ("S", p, i)
                        claim(fr, u, ("K", p))
                        if i == 0:
                            pe.sem_inc(passed_pe, 1)
                        cols = slice(START[i], START[i] + SIZE[i])
                        n = SEEN[i] + SEEN[i] % 2
                        wide = i == NT - 1
                        parts = [(0, HT), (HT, TP)] if wide else [(0, max(n, 256) if i else n)]
                        for s, (lo, hi) in enumerate(parts):
                            for a, m in ((qk_hi, qk_hi), (qk_hi, qk_lo), (qk_lo, qk_hi)):
                                for h in range(2):
                                    rows = slice(64 * h, 64 * h + 64)
                                    bank = 2 * h + s if wide else fr.banks[u][h]
                                    mm = nc.tensor.matmul(work[0:SIZE[i], bank, 0:hi - lo],
                                                          a[rows, p % 2, 0, cols], m[rows, p % 2, 1, lo:hi],
                                                          start=(a is qk_hi and m is qk_hi), stop=(a is qk_lo))
                        mm.then_inc(unit_ready, 1)

                    def turn_p(b, p, j):
                        at_pair = b * NPAIR + p
                        for h in range(2):
                            pe.wait_ge(turn_done[h], 1 + at_pair * NTURN + j)
                            for i in reversed(range(max(j, 1), NT)):
                                if j == 0 and i in (NT - 1, 1):
                                    if (min(i, 2), h) == BY_DVE:
                                        pe.wait_ge(norm_dve_done, at_pair + 1)
                                    else:
                                        pe.wait_ge(norm_done, at_pair * len(BY_POOL) + BY_POOL.index((min(i, 2), h)) + 1)
                                    pe.sem_inc(passed_pe, 1)
                                at = (i - max(j, 1)) * 128
                                mm = nc.tensor.transpose(
                                    turned[h][0:SIZE[j], at:at + 128],
                                    prob[:, p % 2, h, P_AT[i] + START[j]:P_AT[i] + START[j] + SIZE[j]],
                                    ident[:, :])
                            mm.then_inc(turn_ready[h], 1)

                    def turn_first(b, p):
                        pe.wait_ge(y_done, 1 + b * NPAIR + p)
                        pe.wait_ge(norm_done, (b * NPAIR + p + 1) * len(BY_POOL))
                        pe.sem_inc(passed_pe, 1)
                        for h in range(2):
                            mm = nc.tensor.transpose(y_first[0:T0, 128 + 64 * h:128 + 64 * h + T0],
                                                     prob[0:T0, p % 2, h, 0:T0], ident[0:T0, 0:T0])
                        mm.then_inc(first0_ready, 1)

                    def weigh(b, p, j):
                        at_pair = b * NPAIR + p
                        if j == 0:
                            pe.wait_ge(y_done, 1 + at_pair)
                        at = START[max(j, 1)] - T0
                        for h in range(2):
                            pe.wait_ge(turn_done[h], 1 + at_pair * NTURN + j + 1)
                        if j == 0:
                            pe.sem_inc(passed_pe, 1)
                        for h in range(2):
                            cols = slice(p * 128 + 64 * h, p * 128 + 64 * h + 64)
                            mm = nc.tensor.matmul(y_text[64 * h:64 * h + 64, at:512], v[0:SIZE[j], j, cols],
                                                  probT[0:SIZE[j], j % 2, h, 0:512 - at],
                                                  start=(j == 0), stop=(j == NT - 1))
                        mm.then_inc(pv_done, 1)

                    def weigh_first(b, p):
                        pe.wait_ge(first0_done, b * NPAIR + p + 1)
                        pe.sem_inc(passed_pe, 1)
                        for h in range(2):
                            cols = slice(p * 128 + 64 * h, p * 128 + 64 * h + 64)
                            mm = nc.tensor.matmul(y_first[64 * h:64 * h + 64, 0:T0], v[0:T0, 0, cols],
                                                  probT0[:, h, :], start=True, stop=True)
                        mm.then_inc(y_ready, 1)

                    def begin(fr):
                        for u in FIRST:
                            if u[0] == "xT":
                                pe.wait_ge(w_lo, len(W_UNITS) - 4 + fr.banks[u][0] + 1)
                                turn_x(fr, "xT", 0, [u[1]])
                                if u[1] == len(TURNS) - 1:
                                    patches(1)
                            elif u[0] == "V":
                                if u == VALUES[0]:
                                    pe.wait_ge(patch_done, B)
                                values(fr, [u])
                            elif u[0] == "S":
                                scores(fr, 0, u[2])
                            else:
                                project(fr, u[0], 0)
                        pe.wait_ge(unit_free, fr.is_free(VALUES[-1]))

                    def body(b, fr, last):
                        for p in range(NPAIR):
                            more = p + 1 < NPAIR or not last
                            nxt = (p + 1) % NPAIR
                            if more and nxt:
                                project(fr, "Q", nxt)
                            turn_p(b, p, 0)
                            if more and nxt == 0:
                                project(fr, "Q", nxt)
                            if more:
                                project(fr, "K", nxt)
                            turn_p(b, p, 1)
                            turn_first(b, p)
                            weigh(b, p, 0)
                            for j in range(NT):
                                if more:
                                    scores(fr, nxt, NT - 1 - j)
                                if j + 2 < NT:
                                    turn_p(b, p, j + 2)
                                if j + 3 < NT:
                                    weigh(b, p, j + 1)
                                elif j + 2 > NT - 1:
                                    weigh(b, p, j)
                            weigh_first(b, p)
                            if p == NPAIR - 2 and not last:
                                turn_x(fr, "xT", norm_no(b, 0))

                        if not last:
                            values(fr, VALUES[:EARLY])
                        for i in range(NT):
                            u = ("O", i)
                            claim(fr, u)
                            pe.wait_ge(y_done, 1 + (b + 1) * NPAIR)
                            if i == 0:
                                pe.wait_ge(wo_in, 16)
                            for p in range(NPAIR):
                                mm = nc.tensor.matmul(work[0:SIZE[i], fr.banks[u][0], 0:C],
                                                      yT[:, p, START[i]:START[i] + SIZE[i]], wo[:, p, :],
                                                      start=(p == 0), stop=(p == NPAIR - 1))
                            mm.then_inc(unit_ready, 1)
                        if not last:
                            values(fr, VALUES[EARLY:])
                        turn_x(fr, "x2T", norm_no(b, 1, last))

                    batches(pe, begin, body)

                @block.scalar
                def _(act):
                    for n, (m, c, half) in enumerate(W_UNITS):
                        act.wait_ge(w_turned, n + 1)
                        nc.scalar.activation(whi[:, m, c, half * 512:(half + 1) * 512], work[:, n % 4, :], ACT.Copy,
                                             scale=Q_SCALE if m == 0 else 1.0).then_inc(w_hi, 1)
                    act.sem_inc(turn_done[0], 1)
                    act.sem_inc(y_done, 1)

                    def upper(fr, u, dst, src):
                        act.wait_ge(unit_ready, fr.is_ready(u))
                        nc.scalar.activation(dst, src, ACT.Copy).then_inc(hi_done, 1)

                    def upper_x(fr, groups=range(len(TURNS))):
                        for g in groups:
                            u = ("xT", g)
                            lo, hi = turned_tokens(g)
                            upper(fr, u, xhi[:, :, lo:hi],
                                  work[:, fr.banks[u][0], :].rearrange("p (c n) -> p c n", c=CC)[:, :, 0:hi - lo])

                    def upper_qk(fr, kind, p):
                        u = (kind, p)
                        upper(fr, u, qk_hi[:, p % 2, "QK".index(kind), :].rearrange("p (s n) -> p s n", s=2),
                              work[:, fr.banks[u][0]:fr.banks[u][0] + 2, 0:HT])

                    def expo(fr, p, i):
                        for h in range(2):
                            act.wait_ge(unit_free, fr.is_free(("S", p, i)) - 1 + h)
                            rows = prob[0:SIZE[i], p % 2, h, P_AT[i]:P_AT[i] + SEEN[i]]
                            nc.scalar.activation(rows, rows, ACT.Exp, scale=-1.0, bias=low[0:SIZE[i], p % 2, i, h:h + 1],
                                                 accum_out=total[0:SIZE[i], p % 2, i, h:h + 1]).then_inc(exp_done, 1)

                    def take_turned(b, p, j):
                        at_pair = b * NPAIR + p
                        act.wait_ge(turn_ready[0], at_pair * NTURN + j + 1)
                        act.wait_ge(pv_done, 1 + at_pair * NT + j - 1)
                        w = 512 - (START[max(j, 1)] - T0)
                        nc.scalar.activation(probT[0:SIZE[j], j % 2, 0, 0:w], turned[0][0:SIZE[j], 0:w],
                                             ACT.Copy).then_inc(turn_done[0], 1)

                    def take_first(b, p):
                        act.wait_ge(first0_ready, b * NPAIR + p + 1)
                        nc.scalar.activation(probT0[:, :, :], y_first[0:T0, 128:256].rearrange(
                            "p (h n) -> p h n", h=2)[:, :, 0:T0], ACT.Copy).then_inc(first0_done, 1)

                    def take_y(b, p):
                        act.wait_ge(y_ready, b * NPAIR + p + 1)
                        nc.scalar.activation(yT[:, p, 0:T0], y_first[:, 0:T0], ACT.Copy)
                        nc.scalar.activation(yT[:, p, T0:T], y_text[:, :], ACT.Copy).then_inc(y_done, 1)

                    def begin(fr):
                        for u in FIRST:
                            if u[0] == "xT":
                                upper_x(fr, [u[1]])
                            elif u[0] == "S":
                                expo(fr, 0, u[2])
                            elif u[0] != "V":
                                upper_qk(fr, u[0], 0)

                    def body(b, fr, last):
                        for p in range(NPAIR):
                            more = p + 1 < NPAIR or not last
                            nxt = (p + 1) % NPAIR
                            if p:
                                take_y(b, p - 1)
                            if more and nxt:
                                upper_qk(fr, "Q", nxt)
                            take_turned(b, p, 0)
                            if more and nxt == 0:
                                upper_qk(fr, "Q", nxt)
                            if more:
                                upper_qk(fr, "K", nxt)
                            take_turned(b, p, 1)
                            take_first(b, p)
                            for j in range(NT):
                                if j + 2 < NT:
                                    take_turned(b, p, j + 2)
                                if more:
                                    expo(fr, nxt, NT - 1 - j)
                            if p == NPAIR - 2 and not last:
                                upper_x(fr)
                        take_y(b, NPAIR - 1)

                    batches(act, begin, body)

                @block.vector
                def _(dve):
                    nc.vector.memset(px[:, :, 0:1, :], 0.0).then_inc(px_zero, 1)
                    nc.vector.memset(px[:, :, T0:65, :], 0.0).then_inc(px_zero, 1)
                    for t in (xhi, xlo):
                        nc.vector.memset(t[:, :, T:TP].bitcast(F32), 0.0).then_inc(pads, 1)
                    nc.vector.memset(var_eps[:, :], 1.0).then_inc(pads, 1)

                    def lower_weights(which):
                        for n, (m, c, half) in enumerate(W_UNITS):
                            if m != which:
                                continue
                            dve.wait_ge(w_hi, n + 1)
                            dst = wlo[:, m, c, half * 512:(half + 1) * 512]
                            top = whi[:, m, c, half * 512:(half + 1) * 512].bitcast(F32)
                            nc.vector.scalar_tensor_tensor(
                                out=dst, in0=work[:, n % 4, :], scalar=Q_SCALE if m == 0 else 1.0,
                                in1=top, op0=ALU.mult, op1=ALU.subtract).then_inc(w_lo, 1)

                    def add_patches(g):
                        dve.wait_ge(patch_ready, g + 1)
                        for side in range(2):
                            at = 64 * side
                            nc.vector.tensor_tensor(first[:, 2 * g + side, :], turned[g][at:at + T0, 0:C],
                                                    extra[:, 0, :], ALU.add).then_inc(patch_done, 1)

                    dve.sem_inc(unit_free, 1)
                    dve.sem_inc(turn_done[1], 1)

                    def h_tile(b, i):
                        if i == 0:
                            return first[:, bass.ds(b, 1), :].rearrange("p a c -> p (a c)")
                        return acc[:, bass.ds(b * (NT - 1) + (i - 1), 1), :].rearrange("p a c -> p (a c)")

                    def stats_of(b, i):
                        nc.vector.bn_stats(stats[0:SIZE[i], i, :], h_tile(b, i)).then_inc(stats_done, 1)

                    def mean_of_all(n):
                        dve.wait_ge(stats_done, (n + 1) * NT)
                        dve.sem_inc(passed_dve, 1)
                        for i in range(NT):
                            nc.vector.bn_aggr(mean_var[0:SIZE[i], i, :], stats[0:SIZE[i], i, :]).then_inc(aggr_done, 1)
                        dve.wait_ge(aggr_done, (n + 1) * NT)
                        nc.vector.tensor_scalar(var_eps[0:T0, 0:1], mean_var[0:T0, 0, 1:2], LN_EPS, None, ALU.add)
                        nc.vector.tensor_scalar(var_eps[:, 1:NT], mean_var[:, 1:NT, 1], LN_EPS, None,
                                                ALU.add).then_inc(eps_done, 1)

                    def xhat_of_all(b, n):
                        dve.wait_ge(rstd_done, n + 1)
                        for i in range(NT):
                            nc.vector.tensor_scalar(xhat[0:SIZE[i], i, :], h_tile(b, i), mean_var[0:SIZE[i], i, 0:1],
                                                    rstd[0:SIZE[i], i:i + 1], ALU.subtract, ALU.mult
                                                    ).then_inc(xhat_done, 1)

                    def lower(fr, u, dst, src, top):
                        dve.wait_ge(hi_done, fr.is_hi(u))
                        nc.vector.tensor_tensor(dst, src, top, ALU.subtract).then_inc(unit_free, 1)

                    def lower_x(fr, groups=range(len(TURNS))):
                        for g in groups:
                            u = ("xT", g)
                            lo, hi = turned_tokens(g)
                            lower(fr, u, xlo[:, :, lo:hi],
                                  work[:, fr.banks[u][0], :].rearrange("p (c n) -> p c n", c=CC)[:, :, 0:hi - lo],
                                  xhi[:, :, lo:hi].bitcast(F32))

                    def lower_qk(fr, kind, p):
                        u = (kind, p)
                        k = "QK".index(kind)
                        lower(fr, u, qk_lo[:, p % 2, k, :].rearrange("p (s n) -> p s n", s=2),
                              work[:, fr.banks[u][0]:fr.banks[u][0] + 2, 0:HT],
                              qk_hi[:, p % 2, k, :].bitcast(F32).rearrange("p (s n) -> p s n", s=2))

                    def take_values(fr, units):
                        for u in units:
                            i, half = u[1:]
                            dve.wait_ge(unit_ready, fr.is_ready(u))
                            nc.vector.tensor_copy(v[0:SIZE[i], i, half * 512:half * 512 + 512],
                                                  banks[fr.banks[u][0]][0:SIZE[i], :]).then_inc(unit_free, 1)

                    def masked(fr, p, i):
                        u = ("S", p, i)
                        dve.wait_ge(unit_ready, fr.is_ready(u))
                        dve.sem_inc(passed_dve, 1)
                        for h in range(2):
                            rows = slice(0, SIZE[i])
                            at = START[-1] - START[i]
                            if i == NT - 1:
                                src = work[rows, 2 * h:2 * h + 2, 0:HT]
                                dst = prob[rows, p % 2, h, P_AT[i]:P_AT[i] + TP].rearrange("p (s n) -> p s n", s=2)
                                m = mask[rows, 0:TP].rearrange("p (s n) -> p s n", s=2)
                            else:
                                src = work[rows, fr.banks[u][h], 0:SEEN[i]]
                                dst = prob[rows, p % 2, h, P_AT[i]:P_AT[i] + SEEN[i]]
                                m = mask[rows, at:at + SEEN[i]]
                            nc.vector.tensor_tensor_reduce(dst, src, m, 1.0, 3.0e38, ALU.add, ALU.min,
                                                           low[rows, p % 2, i, h:h + 1]).then_inc(unit_free, 1)

                    def shares(b, p, i):
                        dve.wait_ge(exp_done, (b * NPAIR + p) * NS + 2 * DOWNWARD.index(i) + 2)
                        nc.vector.reciprocal(share[0:SIZE[i], p % 2, i, :],
                                             total[0:SIZE[i], p % 2, i, :]).then_inc(share_done, 1)

                    def norm_one(b, p):
                        i, h = BY_DVE
                        rows = prob[0:SIZE[i], p % 2, h, P_AT[i]:P_AT[i] + SEEN[i]]
                        dve.wait_ge(share_done, (b * NPAIR + p) * NT + DOWNWARD.index(i) + 1)
                        nc.vector.tensor_scalar(rows, rows, share[0:SIZE[i], p % 2, i, h:h + 1], None,
                                                ALU.mult).then_inc(norm_dve_done, 1)

                    def take_turned(b, p, j):
                        at_pair = b * NPAIR + p
                        dve.wait_ge(turn_ready[1], at_pair * NTURN + j + 1)
                        dve.wait_ge(pv_done, 1 + at_pair * NT + j - 1)
                        w = 512 - (START[max(j, 1)] - T0)
                        nc.vector.tensor_copy(probT[0:SIZE[j], j % 2, 1, 0:w],
                                              turned[1][0:SIZE[j], 0:w]).then_inc(turn_done[1], 1)

                    def begin(fr):
                        lower_weights(0)
                        dve.wait_ge(extra_in, 48)
                        nc.vector.tensor_tensor(extra[:, 0, :], extra[:, 0, :], extra[:, 1, :], ALU.add).then_inc(extra_done, 1)
                        dve.wait_ge(extra_done, 1)
                        dve.wait_ge(txt0_in, 16)
                        for i in range(1, NT):
                            stats_of(0, i)
                        add_patches(0)
                        dve.wait_ge(patch_done, 2)
                        stats_of(0, 0)
                        dve.wait_ge(pads, 3)
                        mean_of_all(0)
                        lower_weights(1)
                        xhat_of_all(0, 0)
                        lower_weights(2)
                        for u in FIRST:
                            if u[0] == "xT":
                                lower_x(fr, [u[1]])
                                if u[1] == len(TURNS) - 1:
                                    add_patches(1)
                            elif u[0] == "V":
                                take_values(fr, [u])
                            elif u[0] == "S":
                                i = u[2]
                                if i == NT - 1:
                                    dve.wait_ge(mask_made, 2)
                                masked(fr, 0, i)
                                if i < NT - 1:
                                    shares(0, 0, i + 1)
                                if i == BY_DVE[0] - 1:
                                    norm_one(0, 0)
                            else:
                                lower_qk(fr, u[0], 0)
                        shares(0, 0, 0)
                        dve.wait_ge(patch_done, B)
                        dve.wait_ge(txt_in, 16 * (B - 1))

                    def body(b, fr, last):
                        for p in range(NPAIR):
                            more = p + 1 < NPAIR or not last
                            nxt = (p + 1) % NPAIR
                            if more and nxt:
                                lower_qk(fr, "Q", nxt)
                            take_turned(b, p, 0)
                            if more and nxt == 0:
                                lower_qk(fr, "Q", nxt)
                            if more:
                                lower_qk(fr, "K", nxt)
                            take_turned(b, p, 1)
                            if p < NT and not last:
                                stats_of(b + 1, p)
                            if p == NPAIR - 3 and not last:
                                mean_of_all(norm_no(b, 0))
                            if p == NPAIR - 2 and not last:
                                xhat_of_all(b + 1, norm_no(b, 0))
                            for j in range(NT):
                                if more:
                                    masked(fr, nxt, NT - 1 - j)
                                if j + 2 < NT:
                                    take_turned(b, p, j + 2)
                                if more and j + 3 < NT:
                                    shares(b, p + 1, NT - 1 - j)
                            if more:
                                shares(b, p + 1, 2)
                                norm_one(b, p + 1)
                                shares(b, p + 1, 1)
                            if more:
                                shares(b, p + 1, 0)
                            if p == NPAIR - 2 and not last:
                                lower_x(fr)

                        if not last:
                            take_values(fr, VALUES[:EARLY])
                        for i in range(NT):
                            u = ("O", i)
                            dve.wait_ge(unit_ready, fr.is_ready(u))
                            nc.vector.tensor_tensor(h_tile(b, i), work[0:SIZE[i], fr.banks[u][0], 0:C], h_tile(b, i),
                                                    ALU.add).then_inc(unit_free, 1)
                            dve.wait_ge(unit_free, fr.is_free(u))
                            dve.sem_inc(passed_dve, 1)
                            stats_of(b, i)
                        n = norm_no(b, 1, last)
                        mean_of_all(n)
                        if not last:
                            take_values(fr, VALUES[EARLY:EARLY + 2])
                        xhat_of_all(b, n)
                        if not last:
                            take_values(fr, VALUES[EARLY + 2:])
                        for g in range(len(TURNS)):
                            u = ("x2T", g)
                            lo, hi = turned_tokens(g)
                            dve.wait_ge(unit_ready, fr.is_ready(u))
                            src = work[:, fr.banks[u][0], :].rearrange("p (c n) -> p c n", c=CC)[:, :, 0:hi - lo]
                            if g == 0:
                                dst = x2T[:, :, bass.ds(b * T0 + REST, T0)]
                            else:
                                dst = x2T[:, :, bass.ds(b * TXT + (lo - T0), hi - lo)]
                            nc.vector.tensor_copy(dst, src).then_inc(unit_free, 1)

                    batches(dve, begin, body)

        with ExitStack() as two:
            def sb(name, shape, dt=F32):
                return two.enter_context(nc.sbuf_tensor(name, shape, dt))

            WE = 2 * CC * F + FT * C
            x2hi = sb("x2hi", [128, CC, NTOK], F32R)
            x2lo = sb("x2lo", [128, CC, NTOK], F32R)
            wraw = sb("wraw", [128, WE])
            wehi = sb("wehi", [128, 2, WE], F32R)
            welo = sb("welo", [128, 2, WE], F32R)
            fhi = sb("fhi", [128, 2, FT, 512], F32R)
            flo = sb("flo", [128, 2, FT, 512], F32R)
            silu = sb("silu", [128, 2, 512])
            fuse = sb("fuse", [128, 2, 512])
            mixed = sb("mixed", [128, 2, C])
            wr = sb("wr", [128, CC, E])
            logitT = sb("logitT", [E, NTOK])
            logit = sb("logit", [128, ND, E])
            pr = sb("pr", [128, ND, E])
            eq = sb("eq", [128, ND, E])
            run = sb("run", [128, ND, E])
            one_hot = sb("one_hot", [128, 2, ND, E])
            gatew = sb("gatew", [128, ND, E])
            wcol = sb("wcol", [128, 2, ND])
            r1 = sb("r1", [128, 8, ND])

            wr_in, moved, raw_in = sem("wr_in"), sem("moved"), sem("raw_in")
            x2_hi, x2_lo = sem("x2_hi"), sem("x2_lo")
            lt_ready, lt_done, l_ready, l_done = (sem(n) for n in ("lt_ready", "lt_done", "l_ready", "l_done"))
            l_zero = sem("l_zero")
            step = sem("step")
            exp_asked, exp_given = sem("exp_asked"), sem("exp_given")
            we_hi, we_lo = sem("we_hi"), sem("we_lo")
            gu_ready, silu_done, fuse_done, fhi_done, flo_done = (
                sem(n) for n in ("gu_ready", "silu_done", "fuse_done", "fhi_done", "flo_done"))
            down_ready, down_done = sem("down_ready"), sem("down_done")
            wcol_done, stored = sem("wcol_done"), sem("stored")
            NC = len(CHUNKS)
            GU_AHEAD, DOWN_AHEAD = 1, 4
            NG = NC * FT
            SPLITS = [(c, lo, hi) for lo, hi in CHUNKS for c in range(CC)]
            dbanks = [turned[0], turned[1], y_text, y_first]

            def acc_of(k):
                if k < B * (NT - 1):
                    return acc[:, k, :]
                return mixed[0:DOWN[k][1], k - B * (NT - 1), :]

            with nc.Block() as block:
                def part(buf, s, what, *at):
                    if what == "down":
                        f = at[0]
                        o = 2 * CC * F + f * C
                        return buf[:, s, o:o + C]
                    c, f = at
                    o = (CC * F if what == "up" else 0) + c * F + f * 128
                    return buf[:, s, o:o + 128]

                @block.sync
                def _(sp):
                    sp.dma_start(wr[:, :, :], w_router.rearrange("(c p) e -> p c e", p=128)).then_inc(wr_in, 16)
                    for b in range(B):
                        dst = mixed[T0 * b:T0 * (b + 1), 0, :] if b < 3 else mixed[0:T0, 1, :]
                        sp.dma_start(dst, first[:, b, :]).then_inc(moved, 16)

                    def load(e):
                        sp.dma_start(wraw[:, 0:CC * F].rearrange("p (c f) -> p c f", c=CC),
                                     w_gate[e].rearrange("(c p) f -> p c f", p=128)).then_inc(raw_in, 16)
                        sp.dma_start(wraw[:, CC * F:2 * CC * F].rearrange("p (c f) -> p c f", c=CC),
                                     w_up[e].rearrange("(c p) f -> p c f", p=128)).then_inc(raw_in, 16)
                        sp.dma_start(wraw[:, 2 * CC * F:].rearrange("p (f d) -> p f d", f=FT),
                                     w_down[e].rearrange("(f p) d -> p f d", p=128)).then_inc(raw_in, 16)

                    load(0)
                    with sp.Fori(0, E - 1) as e:
                        sp.wait_ge(we_lo, e + 1)
                        load(e + 1)
                    last = (E - 1) * ND
                    order = [k for c in range(NC) for k in chunk_tiles(c)]
                    for n, k in enumerate(order):
                        sp.wait_ge(down_done, DOWN_AHEAD + last + n + 1)
                        if k < B * (NT - 1):
                            b, i = k // (NT - 1), k % (NT - 1)
                            sp.dma_start(out[b, T0 + 128 * i:T0 + 128 * i + 128, :], acc[:, k, :]).then_inc(stored, 16)
                        elif k == B * (NT - 1):
                            for b in range(3):
                                sp.dma_start(out[b, 0:T0, :], mixed[T0 * b:T0 * (b + 1), 0, :]).then_inc(stored, 16)
                        else:
                            sp.dma_start(out[3, 0:T0, :], mixed[0:T0, 1, :]).then_inc(stored, 16)
                    sp.wait_ge(stored, 16 * (B * (NT - 1) + B))

                def tiles_before(c):
                    return sum(len(chunk_tiles(k)) for k in range(c))

                def experts(eng, body):
                    with eng.Fori(0, E // 2 - 1) as pair:
                        for s in range(2):
                            body(pair * 2 + s, s, False)
                    for s in range(2):
                        body(E - 2 + s, s, s == 1)

                STEPS = [(c + 1, c) for c in range(NC - 1)] + [(NC, NC - 1)]

                @block.tensor
                def _(pe):
                    pe.sem_inc(down_ready, 1)
                    pe.wait_ge(wr_in, 16)
                    for n, (lo, hi) in enumerate(CHUNKS):
                        if n >= 2:
                            pe.wait_ge(lt_done, n - 1)
                        for c in range(CC):
                            mm = nc.tensor.matmul(dbanks[2 + n % 2][0:E, 0:hi - lo], wr[:, c, :], x2T[:, c, lo:hi],
                                                  start=(c == 0), stop=(c == CC - 1))
                        mm.then_inc(lt_ready, 1)
                    pe.wait_ge(lt_done, NC)
                    for k, (at, rows) in enumerate(DOWN):
                        mm = nc.tensor.transpose(turned[0][0:rows, k * E:k * E + E], logitT[:, at:at + rows],
                                                 ident[0:E, 0:E])
                    mm.then_inc(l_ready, 1)

                    def gate_up(e, s, c, f):
                        lo, hi = CHUNKS[c]
                        bank = 2 * ((c * FT + f) % 2)
                        if not (isinstance(e, int) and e == 0 and c * FT + f == 0):
                            pe.wait_ge(fuse_done, GU_AHEAD + e * NG + c * FT + f - 1)
                        for w, what in enumerate(("gate", "up")):
                            dst = work[:, bank + w, 0:hi - lo]
                            for k in range(CC):
                                wh, wl = part(wehi, s, what, k, f), part(welo, s, what, k, f)
                                xh, xl = x2hi[:, k, lo:hi], x2lo[:, k, lo:hi]
                                nc.tensor.matmul(dst, wh, xh, start=(k == 0), stop=False)
                                nc.tensor.matmul(dst, wh, xl, start=False, stop=False)
                                mm = nc.tensor.matmul(dst, wl, xh, start=False, stop=(k == CC - 1))
                        mm.then_inc(gu_ready, 1)

                    def down(e, s, c, t):
                        at, rows = DOWN[chunk_tiles(c)[t]]
                        off = at - CHUNKS[c][0]
                        n = tiles_before(c) + t
                        if t == 0:
                            pe.wait_ge(flo_done, e * NG + (c + 1) * FT)
                        pe.wait_ge(down_done, DOWN_AHEAD + e * ND + n - 3)
                        dst = dbanks[(s * ND + n) % 4][0:rows, 0:C]
                        for f in range(FT):
                            fh, fl = (x[:, (s * NC + c) % 2, f, off:off + rows] for x in (fhi, flo))
                            dh, dl = part(wehi, s, "down", f), part(welo, s, "down", f)
                            nc.tensor.matmul(dst, fh, dh, start=(f == 0), stop=False)
                            nc.tensor.matmul(dst, fh, dl, start=False, stop=False)
                            mm = nc.tensor.matmul(dst, fl, dh, start=False, stop=(f == FT - 1))
                        mm.then_inc(down_ready, 1)

                    def body(e, s, last):
                        for c, before in STEPS:
                            tiles = len(chunk_tiles(before))
                            if c == NC and last:
                                for t in range(tiles):
                                    down(e, s, before, t)
                                continue
                            if c == NC:
                                pe.wait_ge(we_lo, e + 2)
                            nxt = (e + 1, 1 - s, 0) if c == NC else (e, s, c)
                            for f in range(FT):
                                gate_up(*nxt, f)
                                if f:
                                    down(e, s, before, f - 1)
                            for t in range(FT - 1, tiles):
                                down(e, s, before, t)

                    pe.wait_ge(x2_lo, len(SPLITS))
                    pe.wait_ge(we_lo, 1)
                    pe.wait_ge(l_done, 3)
                    for f in range(FT):
                        gate_up(0, 0, 0, f)
                    experts(pe, body)

                @block.scalar
                def _(act):
                    for n, (c, lo, hi) in enumerate(SPLITS):
                        nc.scalar.activation(x2hi[:, c, lo:hi], x2T[:, c, lo:hi], ACT.Copy).then_inc(x2_hi, 1)

                    def weights_upper(e, s):
                        act.wait_ge(raw_in, e * 48 + 48)
                        nc.scalar.activation(wehi[:, s, :], wraw[:, :], ACT.Copy).then_inc(we_hi, 1)

                    weights_upper(0, 0)
                    act.wait_ge(exp_asked, 1)
                    nc.scalar.activation(pr[:, :, :], pr[:, :, :], ACT.Exp).then_inc(exp_given, 1)
                    act.wait_ge(exp_asked, 2)
                    nc.scalar.activation(r1[:, 3, :], r1[:, 2, :], ACT.Exp).then_inc(exp_given, 1)

                    def gate(e, s, c, f):
                        n = c * FT + f
                        w = CHUNKS[c][1] - CHUNKS[c][0]
                        act.wait_ge(gu_ready, e * NG + n + 1)
                        nc.scalar.activation(silu[:, n % 2, 0:w], work[:, 2 * (n % 2), 0:w],
                                             ACT.Silu).then_inc(silu_done, 1)

                    def upper(e, s, c, f):
                        n = c * FT + f
                        w = CHUNKS[c][1] - CHUNKS[c][0]
                        act.wait_ge(fuse_done, GU_AHEAD + e * NG + n + 1)
                        nc.scalar.activation(fhi[:, (s * NC + c) % 2, f, 0:w], fuse[:, n % 2, 0:w],
                                             ACT.Copy).then_inc(fhi_done, 1)

                    def body(e, s, last):
                        for c, before in STEPS:
                            if c == NC and last:
                                upper(e, s, before, FT - 1)
                                continue
                            nxt = (e + 1, 1 - s, 0) if c == NC else (e, s, c)
                            for f in range(FT):
                                gate(*nxt, f)
                                if f == 0:
                                    upper(e, s, before, FT - 1)
                                    act.wait_ge(down_ready, 1 + e * ND + tiles_before(c - 1))
                                else:
                                    upper(*nxt, f - 1)
                            if c == 2 and not last:
                                weights_upper(e + 1, 1 - s)

                    for f in range(FT):
                        gate(0, 0, 0, f)
                        if f:
                            upper(0, 0, 0, f - 1)
                    experts(act, body)

                @block.vector
                def _(dve):
                    nc.vector.memset(logit[:, :, :], 0.0).then_inc(l_zero, 1)
                    dve.sem_inc(fuse_done, GU_AHEAD)
                    dve.sem_inc(down_done, DOWN_AHEAD)

                    def take_logits(n):
                        lo, hi = CHUNKS[n]
                        dve.wait_ge(lt_ready, n + 1)
                        nc.vector.tensor_copy(logitT[:, lo:hi], dbanks[2 + n % 2][0:E, 0:hi - lo]).then_inc(lt_done, 1)

                    for n, (c, lo, hi) in enumerate(SPLITS):
                        dve.wait_ge(x2_hi, n + 1)
                        nc.vector.tensor_tensor(x2lo[:, c, lo:hi], x2T[:, c, lo:hi], x2hi[:, c, lo:hi].bitcast(F32),
                                                ALU.subtract).then_inc(x2_lo, 1)
                        if n % 2:
                            take_logits(n // 2)

                    def weights_lower(e, s):
                        dve.wait_ge(we_hi, e + 1)
                        nc.vector.tensor_tensor(welo[:, s, :], wraw[:, :], wehi[:, s, :].bitcast(F32),
                                                ALU.subtract).then_inc(we_lo, 1)

                    dve.wait_ge(l_ready, 1)
                    dve.wait_ge(l_zero, 1)
                    full = B * (NT - 1)
                    bank = turned[0][:, 0:ND * E].rearrange("p (k e) -> p k e", e=E)
                    for rows, a, b in ((128, 0, full), (X_ROWS, full, full + 1), (T0, full + 1, ND)):
                        nc.vector.tensor_copy(logit[0:rows, a:b, :], bank[0:rows, a:b, :]).then_inc(l_done, 1)
                    dve.wait_ge(l_done, 3)
                    weights_lower(0, 0)

                    links = [0]

                    def link(ins):
                        ins.then_inc(step, 1)
                        links[0] += 1
                        dve.wait_ge(step, links[0])

                    def spread(a):
                        return a.unsqueeze(2).to_broadcast([128, ND, E])

                    link(nc.vector.tensor_reduce(r1[:, 0, :], logit[:, :, :], AX.X, ALU.max))
                    nc.vector.tensor_tensor(pr[:, :, :], logit[:, :, :], spread(r1[:, 0, :]),
                                            ALU.subtract).then_inc(exp_asked, 1)
                    dve.wait_ge(exp_given, 1)
                    link(nc.vector.tensor_reduce(r1[:, 7, :], pr[:, :, :], AX.X, ALU.add))
                    link(nc.vector.reciprocal(r1[:, 0, :], r1[:, 7, :]))
                    link(nc.vector.tensor_tensor(pr[:, :, :], pr[:, :, :], spread(r1[:, 0, :]), ALU.mult))

                    def highest(n, to):
                        link(nc.vector.tensor_reduce(r1[:, to, :], pr[:, :, :], AX.X, ALU.max))
                        link(nc.vector.tensor_tensor(eq[:, :, :], pr[:, :, :], spread(r1[:, to, :]), ALU.is_equal))
                        link(nc.vector.tensor_copy(run[:, :, 0], eq[:, :, 0]))
                        for k in range(1, E):
                            link(nc.vector.tensor_tensor(run[:, :, k], run[:, :, k - 1], eq[:, :, k], ALU.add))
                        link(nc.vector.scalar_tensor_tensor(out=one_hot[:, n, :, :], in0=run[:, :, :], scalar=1.0,
                                                            in1=eq[:, :, :], op0=ALU.is_equal, op1=ALU.mult))

                    highest(0, 1)
                    link(nc.vector.scalar_tensor_tensor(out=pr[:, :, :], in0=one_hot[:, 0, :, :], scalar=-2.0,
                                                        in1=pr[:, :, :], op0=ALU.mult, op1=ALU.add))
                    highest(1, 4)
                    nc.vector.tensor_tensor(r1[:, 2, :], r1[:, 4, :], r1[:, 1, :], ALU.subtract).then_inc(exp_asked, 1)
                    dve.wait_ge(exp_given, 2)
                    link(nc.vector.tensor_scalar(r1[:, 5, :], r1[:, 3, :], 1.0, None, ALU.add))
                    link(nc.vector.reciprocal(r1[:, 6, :], r1[:, 5, :]))
                    link(nc.vector.tensor_tensor(r1[:, 7, :], r1[:, 3, :], r1[:, 6, :], ALU.mult))
                    link(nc.vector.tensor_tensor(gatew[:, :, :], one_hot[:, 0, :, :], spread(r1[:, 6, :]), ALU.mult))
                    link(nc.vector.tensor_tensor(run[:, :, :], one_hot[:, 1, :, :], spread(r1[:, 7, :]), ALU.mult))
                    link(nc.vector.tensor_tensor(gatew[:, :, :], gatew[:, :, :], run[:, :, :], ALU.add))
                    dve.wait_ge(moved, 16 * B)

                    def fused(e, s, c, f):
                        n = c * FT + f
                        w = CHUNKS[c][1] - CHUNKS[c][0]
                        if not (isinstance(e, int) and e == 0 and n < 2):
                            dve.wait_ge(flo_done, e * NG + n - 1)
                        dve.wait_ge(silu_done, e * NG + n + 1)
                        nc.vector.tensor_tensor(fuse[:, n % 2, 0:w], work[:, 2 * (n % 2) + 1, 0:w],
                                                silu[:, n % 2, 0:w], ALU.mult).then_inc(fuse_done, 1)

                    def lower(e, s, c, f):
                        n = c * FT + f
                        w = CHUNKS[c][1] - CHUNKS[c][0]
                        fs = (s * NC + c) % 2
                        dve.wait_ge(fhi_done, e * NG + n + 1)
                        nc.vector.tensor_tensor(flo[:, fs, f, 0:w], fuse[:, n % 2, 0:w],
                                                fhi[:, fs, f, 0:w].bitcast(F32), ALU.subtract).then_inc(flo_done, 1)

                    def add(e, s, c, t):
                        k = chunk_tiles(c)[t]
                        rows = DOWN[k][1]
                        n = tiles_before(c) + t
                        dve.wait_ge(down_ready, 1 + e * ND + n + 1)
                        dst = acc_of(k)
                        nc.vector.scalar_tensor_tensor(out=dst, in0=dbanks[(s * ND + n) % 4][0:rows, 0:C],
                                                       scalar=wcol[0:rows, s, k:k + 1], in1=dst,
                                                       op0=ALU.mult, op1=ALU.add).then_inc(down_done, 1)

                    def body(e, s, last):
                        nc.vector.tensor_copy(wcol[:, s, :], gatew[:, :, bass.ds(e, 1)].rearrange("p k a -> p (k a)")
                                              ).then_inc(wcol_done, 1)
                        dve.wait_ge(wcol_done, e + 1)
                        for c, before in STEPS:
                            tiles = len(chunk_tiles(before))
                            if c == NC and last:
                                lower(e, s, before, FT - 1)
                                for t in range(tiles):
                                    add(e, s, before, t)
                                continue
                            nxt = (e + 1, 1 - s, 0) if c == NC else (e, s, c)
                            for f in range(FT):
                                fused(*nxt, f)
                                if f == 0:
                                    lower(e, s, before, FT - 1)
                                else:
                                    lower(*nxt, f - 1)
                                if f >= 2:
                                    add(e, s, before, f - 2)
                            for t in range(FT - 2, tiles):
                                add(e, s, before, t)
                            if c == 2 and not last:
                                weights_lower(e + 1, 1 - s)

                    for f in range(FT):
                        fused(0, 0, 0, f)
                        if f:
                            lower(0, 0, 0, f - 1)
                    experts(dve, body)
    return nc


_INS = ["x", "txt", "L0_tok_W", "L0_tok_b", "L0_tok_cls_token", "L0_tok_pos_emb", "L0_attn_w_q", "L0_attn_w_k",
        "L0_attn_w_v", "L0_attn_w_o", "L0_ffn_kernel_router_DE", "L0_ffn_kernel_gating_EDF",
        "L0_ffn_kernel_up_EDF", "L0_ffn_kernel_down_EFD"]


def kernel(**inputs):
    import numpy as np
    import concourse.bacc as bacc
    from concourse.bass_utils import run_bass_kernel_spmd

    nc = bacc.Bacc("TRN2", target_bir_lowering=False, num_devices=1)
    arrays, args = {}, []
    for name in _INS:
        a = np.ascontiguousarray(inputs[name])
        arrays[f"in_{name}"] = a
        args.append(nc.dram_tensor(f"in_{name}", a.shape, mybir.dt.from_np(a.dtype), kind="ExternalInput").ap())
    args.append(nc.dram_tensor("out", (B, T, C), F32, kind="ExternalOutput").ap())
    fusion_block_kernel(nc, *args)
    r = run_bass_kernel_spmd(nc, [arrays], core_ids=[0])
    return r.results[0]["out"]
```

```python
from contextlib import ExitStack

import concourse.bass as bass
from concourse import mybir

F32 = mybir.dt.float32
F32R = mybir.dt.float32r
ALU = mybir.AluOpType
ACT = mybir.ActivationFunctionType
AX = mybir.AxisListType

B, CH, IMG, P = 4, 3, 96, 16
C = 256
CC = C // 128
G = IMG // P
NP = G * G
TXT = 512
T0 = NP + 1
NT = 1 + TXT // 128
T = T0 + TXT
TP = 552
HT = TP // 2
H, D = 16, 64
HD = H * D
NPAIR = H // 2
E, F = 8, 512
FT = F // 128
WE = 2 * CC * F + FT * C
PIECES = [(k, min(k + 512, WE)) for k in range(0, WE, 512)]
LN_EPS = 1e-5
Q_SCALE = -1.0 / D ** 0.5
MASKED = 1e30

SIZE = [T0] + [128] * (NT - 1)
START = [0] + [T0 + 128 * i for i in range(NT - 1)]
SEEN = [START[i] + SIZE[i] for i in range(NT)]
P_AT = [sum(SEEN[:i]) for i in range(NT)]
P_LEN = P_AT[-1] + TP

NTOK = B * T
REST = B * TXT
CHUNKS = [(0, 512), (512, 1024), (1024, 1536), (1536, 1920), (1920, NTOK)]
X_ROWS = 3 * T0
DOWN = [(128 * k, 128) for k in range(B * (NT - 1))] + [(REST, X_ROWS), (REST + X_ROWS, T0)]
ND = len(DOWN)


def chunk_tiles(c):
    lo, hi = CHUNKS[c]
    return [k for k, (at, _) in enumerate(DOWN) if lo <= at < hi]


NTURN = NT
NS = NT * 2
DOWNWARD = tuple(reversed(range(NT)))
BY_DVE = (2, 1)
BY_POOL = [(i, h) for i in DOWNWARD for h in range(2) if (i, h) != BY_DVE]
TURNS = [range(0, 1), range(1, 3), range(3, 5)]
STARTED = [("xT", g) for g in range(len(TURNS))] + [("Q", 0), ("K", 0)] + [("S", 0, i) for i in DOWNWARD]
EARLY = 4
VALUES = [("V", i, half) for i in range(NT) for half in range(2)]
FIRST = STARTED[:len(TURNS) + 2] + [u for k, i in enumerate(DOWNWARD) for u in VALUES[2 * k:2 * k + 2] + [("S", 0, i)]]
ENDED = [("x2T", g) for g in range(len(TURNS))]


def turned_tokens(g):
    return START[TURNS[g][0]], START[TURNS[g][-1]] + SIZE[TURNS[g][-1]]


class Frame:

    def __init__(self, units, ready, free, hi, held={}, values_apart=False):
        self.units, self.ready0, self.free0, self.hi0 = units, ready, free, hi
        self.banks, self.number, self.before, self.freed, self.hi = {}, {}, {}, {}, {}
        turn = count = 0
        last = dict(held)
        for n, u in enumerate(units):
            if u[0] == "S":
                self.banks[u] = [0, 1, 2, 3] if u[2] == NT - 1 else [0, 1] if u[2] % 2 else [2, 3]
            elif u[0] in "QK":
                self.banks[u] = [0, 1] if u[0] == "Q" else [2, 3]
            elif u[0] == "xT":
                self.banks[u] = [u[1]]
            elif u[0] == "x2T":
                self.banks[u] = [[3, 0, 2][u[1]]]
            elif values_apart and u[0] == "V":
                self.banks[u] = [4 + VALUES.index(u) % 4]
            else:
                self.banks[u] = [turn % 4]
                turn += 1
            if u[0] in ("xT", "Q", "K"):
                self.hi[u] = len(self.hi) + 1
            self.number[u] = n + 1
            self.before[u] = max([last.get(b, -free) for b in self.banks[u]])
            count += 2 if u[0] == "S" else 1
            self.freed[u] = count
            for b in self.banks[u]:
                last[b] = count - (len(self.banks[u]) == 4 and b < 2)
        self.n_ready, self.n_free, self.n_hi = len(units), count, len(self.hi)
        self.left = {b: n - count for b, n in last.items()}

    def is_ready(self, u):
        return self.ready0 + self.number[u]

    def is_free(self, u):
        return self.free0 + self.freed[u]

    def is_hi(self, u):
        return self.hi0 + self.hi[u]


def batch_units(last):
    units = []
    for p in range(1, NPAIR):
        units += [("Q", p), ("K", p)] + [("S", p, i) for i in DOWNWARD]
    if not last:
        units += STARTED + VALUES[:EARLY]
    units += [("O", i) for i in range(NT)]
    return units + ([] if last else VALUES[EARLY:]) + ENDED


def fusion_block_kernel(nc, x, txt, tok_w, tok_b, cls_token, pos_emb, w_q, w_k, w_v, w_o,
                        w_router, w_gate, w_up, w_down, out):
    ctx = ExitStack()
    with ctx:
        def sem(name):
            return ctx.enter_context(nc.semaphore(name))

        def keep(name, shape, dt=F32):
            return ctx.enter_context(nc.sbuf_tensor(name, shape, dt))

        acc = keep("acc", [128, B * (NT - 1), C])
        first = keep("first", [T0, B, C])
        x2T = keep("x2T", [128, CC, NTOK])
        ident = keep("ident", [128, 128])
        wr = keep("wr", [128, CC, E])
        weights_a = keep("weights_a", [128, 3 * CC * HD], F32R)
        weights_b = keep("weights_b", [128, 3 * CC * HD], F32R)
        wehi, welo = ([w[:, s * WE:(s + 1) * WE] for s in range(2)] for w in (weights_a, weights_b))
        v_mem = keep("v_mem", [128, NT * HD])
        wraw = v_mem[:, 0:WE]
        we_raw_in, we_hi, we_lo = sem("we_raw_in"), sem("we_hi"), sem("we_lo")
        wr_in = sem("wr_in")
        work = ctx.enter_context(nc.psum_tensor("work", [128, 4, 512], F32))
        turned = [ctx.enter_context(nc.psum_tensor(f"turned{h}", [128, 512], F32)) for h in range(2)]
        y_text = ctx.enter_context(nc.psum_tensor("y_text", [128, 512], F32))
        y_first = ctx.enter_context(nc.psum_tensor("y_first", [128, 512], F32))
        banks = [work[:, k, :] for k in range(4)] + [turned[0], turned[1], y_text, y_first]

        def load_expert(sp, e):
            sp.dma_start(wraw[:, 0:CC * F].rearrange("p (c f) -> p c f", c=CC),
                         w_gate[e].rearrange("(c p) f -> p c f", p=128)).then_inc(we_raw_in, 16)
            sp.dma_start(wraw[:, CC * F:2 * CC * F].rearrange("p (c f) -> p c f", c=CC),
                         w_up[e].rearrange("(c p) f -> p c f", p=128)).then_inc(we_raw_in, 16)
            sp.dma_start(wraw[:, 2 * CC * F:].rearrange("p (f d) -> p f d", f=FT),
                         w_down[e].rearrange("(f p) d -> p f d", p=128)).then_inc(we_raw_in, 16)

        def split_upper(act, e, s, k):
            lo, hi = PIECES[k]
            act.wait_ge(we_raw_in, e * 48 + 48)
            nc.scalar.activation(wehi[s][:, lo:hi], wraw[:, lo:hi], ACT.Copy).then_inc(we_hi, 1)

        def split_lower(eng, e, s, k):
            lo, hi = PIECES[k]
            eng.wait_ge(we_hi, e * len(PIECES) + k + 1)
            eng.tensor_tensor(welo[s][:, lo:hi], wraw[:, lo:hi], wehi[s][:, lo:hi].bitcast(F32),
                              ALU.subtract).then_inc(we_lo, 1)

        with ExitStack() as one:
            def sb(name, shape, dt=F32):
                return one.enter_context(nc.sbuf_tensor(name, shape, dt))

            whi, wlo = (w[:, :].rearrange("p (m c n) -> p m c n", m=3, c=CC) for w in (weights_a, weights_b))
            wohi = sb("wohi", [128, NPAIR * C], F32R)
            wolo = sb("wolo", [128, NPAIR * C], F32R)
            xhi = sb("xhi", [128, CC, TP], F32R)
            xlo = sb("xlo", [128, CC, TP], F32R)
            v = v_mem[:, :].rearrange("p (t n) -> p t n", t=NT)
            prob = sb("prob", [128, 2, 2, P_LEN])
            probT = sb("probT", [128, 2, 2, 512])
            probT0 = sb("probT0", [T0, 2, T0])
            yT = sb("yT", [128, NPAIR, TP])
            qk_hi = sb("qk_hi", [128, 2, 2, TP], F32R)
            qk_lo = sb("qk_lo", [128, 2, 2, TP], F32R)
            yhi, ylo = ([q[:, :, :, :].rearrange("p a b n -> p (a b n)")[:, k * HD:(k + 1) * HD].rearrange(
                "p (a n) -> p a n", a=NPAIR) for k in range(2)] for q in (qk_hi, qk_lo))
            xhat = sb("xhat", [128, NT, C])
            mask = sb("mask", [128, TP + START[-1]])
            low = sb("low", [128, 2, NT, 2])
            total = sb("total", [128, 2, NT, 2])
            share = sb("share", [128, 2, NT, 2])
            stats = sb("stats", [128, NT, 6])
            mean_var = sb("mean_var", [128, NT, 2])
            var_eps = sb("var_eps", [128, NT])
            rstd = sb("rstd", [128, NT])
            minus_half = sb("minus_half", [128, NT])
            pflat = prob[:, :, :, :].rearrange("p a h n -> p (a h n)")
            raw = [pflat[:, 0:8 * C].rearrange("p (r c) -> p r c", r=8),
                   pflat[:, 8 * C:16 * C].rearrange("p (r c) -> p r c", r=8),
                   yT[:, :, :].rearrange("p a n -> p (a n)")[:, 0:8 * C].rearrange("p (r c) -> p r c", r=8)]
            wo_raw = yT[:, :, :].rearrange("p a n -> p (a n)")[:, 8 * C:16 * C]
            extra = pflat[0:T0, 16 * C:18 * C].rearrange("p (a c) -> p a c", a=2)
            KP, DX = CH * P, P // 2
            tokw = v[0:2 * KP, :, :].rearrange("p a n -> p (a n)")[:, 0:DX * C].rearrange("p (d e) -> p d e", d=DX)
            COLS = 64 + T0
            px = x2T[0:2 * KP, :, :].rearrange("p a n -> p (a n)")[:, 0:2 * COLS * P].rearrange(
                "p (g s d) -> p g s d", g=2, d=P)

            w_in = [sem(f"w_in{m}") for m in range(3)]
            px_in = [sem(f"px_in{g}") for g in range(2)]
            px_shifted = [sem(f"px_shifted{g}") for g in range(2)]
            wo_in, tokw_in, extra_in, txt0_in, txt_in = (sem(n) for n in ("wo_in", "tokw_in", "extra_in", "txt0_in", "txt_in"))
            ident_made, mask_made, half_made = sem("ident_made"), sem("mask_made"), sem("half_made")
            px_zero = sem("px_zero")
            pads = sem("pads")
            w_turned, w_hi, w_lo = sem("w_turned"), sem("w_hi"), sem("w_lo")
            patch_ready, patch_done, extra_done = sem("patch_ready"), sem("patch_done"), sem("extra_done")
            unit_ready, unit_free = sem("unit_ready"), sem("unit_free")
            hi_done = sem("hi_done")
            stats_done, aggr_done, eps_done, rstd_done, xhat_done = (
                sem(n) for n in ("stats_done", "aggr_done", "eps_done", "rstd_done", "xhat_done"))
            exp_done, share_done, norm_done, norm_dve_done = (
                sem(n) for n in ("exp_done", "share_done", "norm_done", "norm_dve_done"))
            turn_ready = [sem(f"turn_ready{h}") for h in range(2)]
            turn_done = [sem(f"turn_done{h}") for h in range(2)]
            pv_done, y_ready, y_done = sem("pv_done"), sem("y_ready"), sem("y_done")
            passed_dve, passed_pe = sem("passed_dve"), sem("passed_pe")
            wo_hi, wo_lo, yhi_done, ylo_done = (sem(n) for n in ("wo_hi", "wo_lo", "yhi_done", "ylo_done"))
            first0_ready, first0_done = sem("first0_ready"), sem("first0_done")

            start = Frame(FIRST, 0, 1, 0, values_apart=True)
            one_batch = Frame(batch_units(False), 0, 0, 0)
            held = {b: max(start.left[b], one_batch.left[b]) for b in range(4)}

            def frame_of(b, last):
                return Frame(batch_units(last), start.n_ready + b * one_batch.n_ready,
                             1 + start.n_free + b * one_batch.n_free, start.n_hi + b * one_batch.n_hi,
                             held)

            def batches(eng, begin, body):
                begin(start)
                with eng.Fori(0, B - 1) as b:
                    body(b, frame_of(b, False), False)
                body(B - 1, frame_of(B - 1, True), True)

            def norm_no(b, which, last=False):
                return 2 * b + (1 if which == 0 or last else 2)

            with nc.Block() as block:
                W_UNITS = [(m, c, half) for m in range(3) for c in range(CC) for half in range(2)]

                @block.sync
                def _(sp):
                    def load_txt(b):
                        sp.dma_start(acc[:, b * (NT - 1):(b + 1) * (NT - 1), :], txt[b].rearrange(
                            "(r p) c -> p r c", p=128)).then_inc(txt_in if b else txt0_in, 16)

                    def load_images(g):
                        for side in range(2):
                            for ch in range(CH):
                                sp.dma_start(
                                    px[ch * P:(ch + 1) * P, g, 64 * side + 1:64 * side + T0, :].rearrange(
                                        "y (r q) d -> y r (q d)", r=G),
                                    x[2 * g + side, ch].rearrange("(r y) w -> y r w", y=P)).then_inc(px_in[g], 16)

                    def shift_images(g):
                        sp.wait_ge(px_in[g], 16 * 2 * CH)
                        flat = px[:, g, :, :].rearrange("k s d -> k (s d)")
                        sp.dma_start(flat[KP:2 * KP, 0:COLS * P - DX], flat[0:KP, DX:COLS * P]).then_inc(px_shifted[g], 16)

                    def load_weights(m, w):
                        sp.dma_start(raw[m], w.rearrange("h d c -> (h d) c").rearrange(
                            "(r p) c -> p r c", p=128)).then_inc(w_in[m], 16)

                    load_weights(0, w_q)
                    sp.wait_ge(px_zero, 2)
                    load_images(0)
                    for half in range(2):
                        for ch in range(CH):
                            row = half * KP + ch * P
                            sp.dma_start(tokw[row:row + P], tok_w.rearrange("(y x c) e -> c y x e", y=P, c=CH)[
                                ch][:, half * DX:half * DX + DX, :]).then_inc(tokw_in, 16)
                    shift_images(0)
                    load_weights(1, w_k)
                    load_txt(0)
                    sp.dma_start(extra[:, 0, :], pos_emb).then_inc(extra_in, 16)
                    sp.dma_start(extra[0:1, 1, :], cls_token.rearrange("a b e -> (a b) e")).then_inc(extra_in, 16)
                    sp.dma_start(extra[1:T0, 1, :], tok_b.rearrange("(a e) -> a e", a=1).to_broadcast([NP, C])
                                 ).then_inc(extra_in, 16)
                    load_weights(2, w_v)
                    load_images(1)
                    shift_images(1)
                    sp.dma_start(wo_raw.rearrange("p (r c) -> p r c", c=C), w_o.rearrange("(r p) c -> p r c", p=128)
                                 ).then_inc(wo_in, 16)
                    for b in range(1, B):
                        load_txt(b)
                    sp.dma_start(wr[:, :, :], w_router.rearrange("(c p) e -> p c e", p=128)).then_inc(wr_in, 16)
                    sp.wait_ge(y_ready, B * NPAIR)
                    load_expert(sp, 0)

                @block.gpsimd
                def _(pool):
                    nc.gpsimd.memset(ident[:, :], 1.0).then_inc(ident_made, 1)
                    pool.wait_ge(ident_made, 1)
                    nc.gpsimd.affine_select(out=ident[:, :], in_=ident[:, :], pattern=[[-1, 128]],
                                            compare_op=ALU.is_equal, fill=0.0, base=0,
                                            channel_multiplier=1).then_inc(ident_made, 1)
                    nc.gpsimd.memset(minus_half[:, :], -0.5).then_inc(half_made, 1)
                    nc.gpsimd.memset(mask[:, :], 0.0).then_inc(mask_made, 1)
                    pool.wait_ge(mask_made, 1)
                    nc.gpsimd.affine_select(out=mask[:, :], in_=mask[:, :], pattern=[[-1, TP + START[-1]]],
                                            compare_op=ALU.is_ge, fill=MASKED, base=START[-1],
                                            channel_multiplier=1).then_inc(mask_made, 1)
                    pool.wait_ge(half_made, 1)

                    def rstd_of(n, lo=0, hi=NT):
                        pool.wait_ge(eps_done, n + 1 + (1 if lo else 0))
                        nc.gpsimd.tensor_tensor(rstd[:, lo:hi], var_eps[:, lo:hi], minus_half[:, lo:hi],
                                                ALU.pow).then_inc(rstd_done, 1)

                    def norm(b, p):
                        for k, i in enumerate(DOWNWARD):
                            pool.wait_ge(share_done, (b * NPAIR + p) * NT + k + 1)
                            for h in [h for h in range(2) if (i, h) in BY_POOL]:
                                rows = prob[0:SIZE[i], p % 2, h, P_AT[i]:P_AT[i] + SEEN[i]]
                                nc.gpsimd.tensor_tensor(
                                    rows, rows, share[0:SIZE[i], p % 2, i, h:h + 1].to_broadcast(
                                        [SIZE[i], SEEN[i]]), ALU.mult).then_inc(norm_done, 1)

                    def begin(fr):
                        rstd_of(0)
                        norm(0, 0)

                    def body(b, fr, last):
                        for p in range(NPAIR):
                            if p + 1 < NPAIR or not last:
                                norm(b, p + 1)
                            if p == NPAIR - 3 and not last:
                                rstd_of(norm_no(b, 0))
                        if last:
                            for k in range(len(PIECES)):
                                split_lower(pool, 0, 0, k)
                            rstd_of(norm_no(b, 1, last), 0, NT - 1)
                            rstd_of(norm_no(b, 1, last), NT - 1, NT)
                        else:
                            rstd_of(norm_no(b, 1))

                    batches(pool, begin, body)

                @block.tensor
                def _(pe):
                    def patches(g):
                        pe.wait_ge(px_shifted[g], 16)
                        for d in range(DX):
                            mm = nc.tensor.matmul(turned[g][0:COLS, 0:C], px[:, g, :, d], tokw[:, d, :],
                                                  start=(d == 0), stop=(d == DX - 1))
                        mm.then_inc(patch_ready, 1)

                    def turn_weights(which):
                        for n, (m, c, half) in enumerate(W_UNITS):
                            if m != which:
                                continue
                            if c == 0 and half == 0:
                                pe.wait_ge(w_in[m], 16)
                            if n >= 4:
                                pe.wait_ge(w_lo, n - 3)
                            for r in range(4):
                                mm = nc.tensor.transpose(work[:, n % 4, r * 128:(r + 1) * 128],
                                                         raw[m][:, 4 * half + r, c * 128:(c + 1) * 128], ident[:, :])
                            mm.then_inc(w_turned, 1)

                    pe.wait_ge(ident_made, 2)
                    turn_weights(0)
                    pe.wait_ge(tokw_in, 16 * 2 * CH)
                    patches(0)
                    turn_weights(1)
                    turn_weights(2)
                    pe.wait_ge(pads, 2)
                    pe.sem_inc(pv_done, 1)

                    def claim(fr, u, after=None):
                        n = max(fr.before[u], fr.freed[after]) if after else fr.before[u]
                        if not (isinstance(fr.free0, int) and fr.free0 + n <= 0):
                            pe.wait_ge(unit_free, fr.free0 + n)

                    def three(dst, a, m, first_, last_):
                        nc.tensor.matmul(dst, a[0], m[0], start=first_, stop=False)
                        nc.tensor.matmul(dst, a[0], m[1], start=False, stop=False)
                        return nc.tensor.matmul(dst, a[1], m[0], start=False, stop=last_)

                    def turn_x(fr, kind, n, groups=range(len(TURNS))):
                        for g in groups:
                            u, tiles = (kind, g), TURNS[g]
                            claim(fr, u)
                            for i in tiles:
                                pe.wait_ge(xhat_done, n * NT + i + 1)
                                if i == 0:
                                    pe.sem_inc(passed_pe, 1)
                                for c in range(CC):
                                    at = c * 256 + (i - tiles[0]) * 128
                                    mm = nc.tensor.transpose(work[:, fr.banks[u][0], at:at + SIZE[i]],
                                                             xhat[0:SIZE[i], i, c * 128:(c + 1) * 128],
                                                             ident[0:SIZE[i], 0:SIZE[i]])
                            mm.then_inc(unit_ready, 1)

                    def values(fr, units):
                        for u in units:
                            i, half = u[1:]
                            claim(fr, u, ("xT", next(g for g, tiles in enumerate(TURNS) if i in tiles)))
                            cols = slice(START[i], START[i] + SIZE[i])
                            n = slice(half * 512, half * 512 + 512)
                            for c in range(CC):
                                mm = three(banks[fr.banks[u][0]][0:SIZE[i], :], (xhi[:, c, cols], xlo[:, c, cols]),
                                           (whi[:, 2, c, n], wlo[:, 2, c, n]), c == 0, c == CC - 1)
                            mm.then_inc(unit_ready, 1)

                    def project(fr, kind, p):
                        u = (kind, p)
                        m = "QK".index(kind)
                        claim(fr, u)
                        rows = slice(p * 128, p * 128 + 128)
                        for s in range(2):
                            if p == 0:
                                pe.wait_ge(unit_free, fr.is_free(("xT", s + 1)))
                            n = slice(s * HT, s * HT + HT)
                            for c in range(CC):
                                mm = three(work[:, fr.banks[u][s], 0:HT], (whi[:, m, c, rows], wlo[:, m, c, rows]),
                                           (xhi[:, c, n], xlo[:, c, n]), c == 0, c == CC - 1)
                        mm.then_inc(unit_ready, 1)

                    def scores(fr, p, i):
                        u = ("S", p, i)
                        claim(fr, u, ("K", p))
                        if i == 0:
                            pe.sem_inc(passed_pe, 1)
                        cols = slice(START[i], START[i] + SIZE[i])
                        n = SEEN[i] + SEEN[i] % 2
                        wide = i == NT - 1
                        parts = [(0, HT), (HT, TP)] if wide else [(0, max(n, 256) if i else n)]
                        for s, (lo, hi) in enumerate(parts):
                            for a, m in ((qk_hi, qk_hi), (qk_hi, qk_lo), (qk_lo, qk_hi)):
                                for h in range(2):
                                    rows = slice(64 * h, 64 * h + 64)
                                    bank = 2 * h + s if wide else fr.banks[u][h]
                                    mm = nc.tensor.matmul(work[0:SIZE[i], bank, 0:hi - lo],
                                                          a[rows, p % 2, 0, cols], m[rows, p % 2, 1, lo:hi],
                                                          start=(a is qk_hi and m is qk_hi), stop=(a is qk_lo))
                        mm.then_inc(unit_ready, 1)

                    def turn_p(b, p, j):
                        at_pair = b * NPAIR + p
                        for h in range(2):
                            pe.wait_ge(turn_done[h], 1 + at_pair * NTURN + j)
                            for i in reversed(range(max(j, 1), NT)):
                                if j == 0 and i in (NT - 1, 1):
                                    if (min(i, 2), h) == BY_DVE:
                                        pe.wait_ge(norm_dve_done, at_pair + 1)
                                    else:
                                        pe.wait_ge(norm_done, at_pair * len(BY_POOL) + BY_POOL.index((min(i, 2), h)) + 1)
                                    pe.sem_inc(passed_pe, 1)
                                at = (i - max(j, 1)) * 128
                                mm = nc.tensor.transpose(
                                    turned[h][0:SIZE[j], at:at + 128],
                                    prob[:, p % 2, h, P_AT[i] + START[j]:P_AT[i] + START[j] + SIZE[j]],
                                    ident[:, :])
                            mm.then_inc(turn_ready[h], 1)

                    def turn_first(b, p):
                        pe.wait_ge(y_done, 1 + b * NPAIR + p)
                        pe.wait_ge(norm_done, (b * NPAIR + p + 1) * len(BY_POOL))
                        pe.sem_inc(passed_pe, 1)
                        for h in range(2):
                            mm = nc.tensor.transpose(y_first[0:T0, 128 + 64 * h:128 + 64 * h + T0],
                                                     prob[0:T0, p % 2, h, 0:T0], ident[0:T0, 0:T0])
                        mm.then_inc(first0_ready, 1)

                    def weigh(b, p, j):
                        at_pair = b * NPAIR + p
                        if j == 0:
                            pe.wait_ge(y_done, 1 + at_pair)
                        at = START[max(j, 1)] - T0
                        for h in range(2):
                            pe.wait_ge(turn_done[h], 1 + at_pair * NTURN + j + 1)
                        if j == 0:
                            pe.sem_inc(passed_pe, 1)
                        for h in range(2):
                            cols = slice(p * 128 + 64 * h, p * 128 + 64 * h + 64)
                            mm = nc.tensor.matmul(y_text[64 * h:64 * h + 64, at:512], v[0:SIZE[j], j, cols],
                                                  probT[0:SIZE[j], j % 2, h, 0:512 - at],
                                                  start=(j == 0), stop=(j == NT - 1))
                        mm.then_inc(pv_done, 1)

                    def weigh_first(b, p):
                        pe.wait_ge(first0_done, b * NPAIR + p + 1)
                        pe.sem_inc(passed_pe, 1)
                        for h in range(2):
                            cols = slice(p * 128 + 64 * h, p * 128 + 64 * h + 64)
                            mm = nc.tensor.matmul(y_first[64 * h:64 * h + 64, 0:T0], v[0:T0, 0, cols],
                                                  probT0[:, h, :], start=True, stop=True)
                        mm.then_inc(y_ready, 1)

                    def begin(fr):
                        for u in FIRST:
                            if u[0] == "xT":
                                pe.wait_ge(w_lo, len(W_UNITS) - 4 + fr.banks[u][0] + 1)
                                turn_x(fr, "xT", 0, [u[1]])
                                if u[1] == len(TURNS) - 1:
                                    patches(1)
                            elif u[0] == "V":
                                if u == VALUES[0]:
                                    pe.wait_ge(patch_done, B)
                                values(fr, [u])
                            elif u[0] == "S":
                                scores(fr, 0, u[2])
                            else:
                                project(fr, u[0], 0)
                        pe.wait_ge(unit_free, fr.is_free(VALUES[-1]))

                    def body(b, fr, last):
                        for p in range(NPAIR):
                            more = p + 1 < NPAIR or not last
                            nxt = (p + 1) % NPAIR
                            if more and nxt:
                                project(fr, "Q", nxt)
                            turn_p(b, p, 0)
                            if more and nxt == 0:
                                project(fr, "Q", nxt)
                            if more:
                                project(fr, "K", nxt)
                            turn_p(b, p, 1)
                            turn_first(b, p)
                            weigh(b, p, 0)
                            for j in range(NT):
                                if more:
                                    scores(fr, nxt, NT - 1 - j)
                                if j + 2 < NT:
                                    turn_p(b, p, j + 2)
                                if j + 3 < NT:
                                    weigh(b, p, j + 1)
                                elif j + 2 > NT - 1:
                                    weigh(b, p, j)
                            weigh_first(b, p)
                            if p == NPAIR - 2 and not last:
                                turn_x(fr, "xT", norm_no(b, 0))

                        if not last:
                            values(fr, VALUES[:EARLY])
                        for i in range(NT):
                            u = ("O", i)
                            claim(fr, u)
                            pe.wait_ge(ylo_done, b * NT + i + 1)
                            if i == 0:
                                pe.wait_ge(wo_lo, NPAIR * C // 512)
                            for p in range(NPAIR):
                                mm = three(work[0:SIZE[i], fr.banks[u][0], 0:C],
                                           (yhi[i % 2][:, p, 0:SIZE[i]], ylo[i % 2][:, p, 0:SIZE[i]]),
                                           (wohi[:, p * C:(p + 1) * C], wolo[:, p * C:(p + 1) * C]),
                                           p == 0, p == NPAIR - 1)
                            mm.then_inc(unit_ready, 1)
                        if not last:
                            values(fr, VALUES[EARLY:])
                        turn_x(fr, "x2T", norm_no(b, 1, last))

                    batches(pe, begin, body)

                @block.scalar
                def _(act):
                    for n, (m, c, half) in enumerate(W_UNITS):
                        act.wait_ge(w_turned, n + 1)
                        nc.scalar.activation(whi[:, m, c, half * 512:(half + 1) * 512], work[:, n % 4, :], ACT.Copy,
                                             scale=Q_SCALE if m == 0 else 1.0).then_inc(w_hi, 1)
                    act.sem_inc(turn_done[0], 1)
                    act.sem_inc(y_done, 1)

                    def upper(fr, u, dst, src):
                        act.wait_ge(unit_ready, fr.is_ready(u))
                        nc.scalar.activation(dst, src, ACT.Copy).then_inc(hi_done, 1)

                    def upper_x(fr, groups=range(len(TURNS))):
                        for g in groups:
                            u = ("xT", g)
                            lo, hi = turned_tokens(g)
                            upper(fr, u, xhi[:, :, lo:hi],
                                  work[:, fr.banks[u][0], :].rearrange("p (c n) -> p c n", c=CC)[:, :, 0:hi - lo])

                    def upper_qk(fr, kind, p):
                        u = (kind, p)
                        upper(fr, u, qk_hi[:, p % 2, "QK".index(kind), :].rearrange("p (s n) -> p s n", s=2),
                              work[:, fr.banks[u][0]:fr.banks[u][0] + 2, 0:HT])

                    def expo(fr, p, i):
                        for h in range(2):
                            act.wait_ge(unit_free, fr.is_free(("S", p, i)) - 1 + h)
                            rows = prob[0:SIZE[i], p % 2, h, P_AT[i]:P_AT[i] + SEEN[i]]
                            nc.scalar.activation(rows, rows, ACT.Exp, scale=-1.0, bias=low[0:SIZE[i], p % 2, i, h:h + 1],
                                                 accum_out=total[0:SIZE[i], p % 2, i, h:h + 1]).then_inc(exp_done, 1)

                    def take_turned(b, p, j):
                        at_pair = b * NPAIR + p
                        act.wait_ge(turn_ready[0], at_pair * NTURN + j + 1)
                        act.wait_ge(pv_done, 1 + at_pair * NT + j - 1)
                        w = 512 - (START[max(j, 1)] - T0)
                        nc.scalar.activation(probT[0:SIZE[j], j % 2, 0, 0:w], turned[0][0:SIZE[j], 0:w],
                                             ACT.Copy).then_inc(turn_done[0], 1)

                    def take_first(b, p):
                        act.wait_ge(first0_ready, b * NPAIR + p + 1)
                        nc.scalar.activation(probT0[:, :, :], y_first[0:T0, 128:256].rearrange(
                            "p (h n) -> p h n", h=2)[:, :, 0:T0], ACT.Copy).then_inc(first0_done, 1)

                    def take_y(b, p):
                        act.wait_ge(y_ready, b * NPAIR + p + 1)
                        nc.scalar.activation(yT[:, p, 0:T0], y_first[:, 0:T0], ACT.Copy)
                        nc.scalar.activation(yT[:, p, T0:T], y_text[:, :], ACT.Copy).then_inc(y_done, 1)

                    def upper_wo(n):
                        k = slice(512 * n, 512 * n + 512)
                        act.wait_ge(wo_in, 16)
                        nc.scalar.activation(wohi[:, k], wo_raw[:, k], ACT.Copy).then_inc(wo_hi, 1)

                    def begin(fr):
                        for u in FIRST:
                            if u[0] == "xT":
                                upper_x(fr, [u[1]])
                            elif u[0] == "S":
                                expo(fr, 0, u[2])
                                if u[2]:
                                    upper_wo(DOWNWARD.index(u[2]))
                            elif u[0] != "V":
                                upper_qk(fr, u[0], 0)
                        act.wait_ge(wo_lo, NPAIR * C // 512)

                    def body(b, fr, last):
                        for p in range(NPAIR):
                            more = p + 1 < NPAIR or not last
                            nxt = (p + 1) % NPAIR
                            if p:
                                take_y(b, p - 1)
                            if more and nxt:
                                upper_qk(fr, "Q", nxt)
                            take_turned(b, p, 0)
                            if more and nxt == 0:
                                upper_qk(fr, "Q", nxt)
                            if more:
                                upper_qk(fr, "K", nxt)
                            take_turned(b, p, 1)
                            take_first(b, p)
                            for j in range(NT):
                                if j + 2 < NT:
                                    take_turned(b, p, j + 2)
                                if more:
                                    expo(fr, nxt, NT - 1 - j)
                            if p == NPAIR - 2 and not last:
                                upper_x(fr)
                        take_y(b, NPAIR - 1)
                        act.wait_ge(y_done, 1 + (b + 1) * NPAIR)
                        for i in range(NT):
                            if i >= 2:
                                act.wait_ge(unit_ready, fr.is_ready(("O", i - 2)))
                            nc.scalar.activation(yhi[i % 2][:, :, 0:SIZE[i]], yT[:, :, START[i]:START[i] + SIZE[i]],
                                                 ACT.Copy).then_inc(yhi_done, 1)
                            if last and i >= 2:
                                for k in range(2 * i - 4, 2 * i - 2):
                                    split_upper(act, 0, 0, k)

                    batches(act, begin, body)

                @block.vector
                def _(dve):
                    nc.vector.memset(px[:, :, 0:1, :], 0.0).then_inc(px_zero, 1)
                    nc.vector.memset(px[:, :, T0:65, :], 0.0).then_inc(px_zero, 1)
                    for t in (xhi, xlo):
                        nc.vector.memset(t[:, :, T:TP].bitcast(F32), 0.0).then_inc(pads, 1)
                    nc.vector.memset(var_eps[:, :], 1.0).then_inc(pads, 1)

                    def lower_weights(which):
                        for n, (m, c, half) in enumerate(W_UNITS):
                            if m != which:
                                continue
                            dve.wait_ge(w_hi, n + 1)
                            dst = wlo[:, m, c, half * 512:(half + 1) * 512]
                            top = whi[:, m, c, half * 512:(half + 1) * 512].bitcast(F32)
                            nc.vector.scalar_tensor_tensor(
                                out=dst, in0=work[:, n % 4, :], scalar=Q_SCALE if m == 0 else 1.0,
                                in1=top, op0=ALU.mult, op1=ALU.subtract).then_inc(w_lo, 1)

                    def add_patches(g):
                        dve.wait_ge(patch_ready, g + 1)
                        for side in range(2):
                            at = 64 * side
                            nc.vector.tensor_tensor(first[:, 2 * g + side, :], turned[g][at:at + T0, 0:C],
                                                    extra[:, 0, :], ALU.add).then_inc(patch_done, 1)

                    dve.sem_inc(unit_free, 1)
                    dve.sem_inc(turn_done[1], 1)

                    def h_tile(b, i):
                        if i == 0:
                            return first[:, bass.ds(b, 1), :].rearrange("p a c -> p (a c)")
                        return acc[:, bass.ds(b * (NT - 1) + (i - 1), 1), :].rearrange("p a c -> p (a c)")

                    def stats_of(b, i):
                        nc.vector.bn_stats(stats[0:SIZE[i], i, :], h_tile(b, i)).then_inc(stats_done, 1)

                    def mean_of(n, lo, hi):
                        dve.wait_ge(stats_done, n * NT + hi)
                        dve.sem_inc(passed_dve, 1)
                        for i in range(lo, hi):
                            nc.vector.bn_aggr(mean_var[0:SIZE[i], i, :], stats[0:SIZE[i], i, :]).then_inc(aggr_done, 1)
                        dve.wait_ge(aggr_done, n * NT + hi)
                        if lo == 0:
                            nc.vector.tensor_scalar(var_eps[0:T0, 0:1], mean_var[0:T0, 0, 1:2], LN_EPS, None, ALU.add)
                        rest = slice(max(lo, 1), hi)
                        nc.vector.tensor_scalar(var_eps[:, rest], mean_var[:, rest, 1], LN_EPS, None,
                                                ALU.add).then_inc(eps_done, 1)

                    def xhat_of(b, n, lo, hi):
                        dve.wait_ge(rstd_done, n + 1 + (1 if lo else 0))
                        for i in range(lo, hi):
                            nc.vector.tensor_scalar(xhat[0:SIZE[i], i, :], h_tile(b, i), mean_var[0:SIZE[i], i, 0:1],
                                                    rstd[0:SIZE[i], i:i + 1], ALU.subtract, ALU.mult
                                                    ).then_inc(xhat_done, 1)

                    def lower(fr, u, dst, src, top):
                        dve.wait_ge(hi_done, fr.is_hi(u))
                        nc.vector.tensor_tensor(dst, src, top, ALU.subtract).then_inc(unit_free, 1)

                    def lower_x(fr, groups=range(len(TURNS))):
                        for g in groups:
                            u = ("xT", g)
                            lo, hi = turned_tokens(g)
                            lower(fr, u, xlo[:, :, lo:hi],
                                  work[:, fr.banks[u][0], :].rearrange("p (c n) -> p c n", c=CC)[:, :, 0:hi - lo],
                                  xhi[:, :, lo:hi].bitcast(F32))

                    def lower_qk(fr, kind, p):
                        u = (kind, p)
                        k = "QK".index(kind)
                        lower(fr, u, qk_lo[:, p % 2, k, :].rearrange("p (s n) -> p s n", s=2),
                              work[:, fr.banks[u][0]:fr.banks[u][0] + 2, 0:HT],
                              qk_hi[:, p % 2, k, :].bitcast(F32).rearrange("p (s n) -> p s n", s=2))

                    def take_values(fr, units):
                        for u in units:
                            i, half = u[1:]
                            dve.wait_ge(unit_ready, fr.is_ready(u))
                            nc.vector.tensor_copy(v[0:SIZE[i], i, half * 512:half * 512 + 512],
                                                  banks[fr.banks[u][0]][0:SIZE[i], :]).then_inc(unit_free, 1)

                    def masked(fr, p, i):
                        u = ("S", p, i)
                        dve.wait_ge(unit_ready, fr.is_ready(u))
                        dve.sem_inc(passed_dve, 1)
                        for h in range(2):
                            rows = slice(0, SIZE[i])
                            at = START[-1] - START[i]
                            if i == NT - 1:
                                src = work[rows, 2 * h:2 * h + 2, 0:HT]
                                dst = prob[rows, p % 2, h, P_AT[i]:P_AT[i] + TP].rearrange("p (s n) -> p s n", s=2)
                                m = mask[rows, 0:TP].rearrange("p (s n) -> p s n", s=2)
                            else:
                                src = work[rows, fr.banks[u][h], 0:SEEN[i]]
                                dst = prob[rows, p % 2, h, P_AT[i]:P_AT[i] + SEEN[i]]
                                m = mask[rows, at:at + SEEN[i]]
                            nc.vector.tensor_tensor_reduce(dst, src, m, 1.0, 3.0e38, ALU.add, ALU.min,
                                                           low[rows, p % 2, i, h:h + 1]).then_inc(unit_free, 1)

                    def shares(b, p, i):
                        dve.wait_ge(exp_done, (b * NPAIR + p) * NS + 2 * DOWNWARD.index(i) + 2)
                        nc.vector.reciprocal(share[0:SIZE[i], p % 2, i, :],
                                             total[0:SIZE[i], p % 2, i, :]).then_inc(share_done, 1)

                    def norm_one(b, p):
                        i, h = BY_DVE
                        rows = prob[0:SIZE[i], p % 2, h, P_AT[i]:P_AT[i] + SEEN[i]]
                        dve.wait_ge(share_done, (b * NPAIR + p) * NT + DOWNWARD.index(i) + 1)
                        nc.vector.tensor_scalar(rows, rows, share[0:SIZE[i], p % 2, i, h:h + 1], None,
                                                ALU.mult).then_inc(norm_dve_done, 1)

                    def take_turned(b, p, j):
                        at_pair = b * NPAIR + p
                        dve.wait_ge(turn_ready[1], at_pair * NTURN + j + 1)
                        dve.wait_ge(pv_done, 1 + at_pair * NT + j - 1)
                        w = 512 - (START[max(j, 1)] - T0)
                        nc.vector.tensor_copy(probT[0:SIZE[j], j % 2, 1, 0:w],
                                              turned[1][0:SIZE[j], 0:w]).then_inc(turn_done[1], 1)

                    def lower_wo(n):
                        k = slice(512 * n, 512 * n + 512)
                        dve.wait_ge(wo_hi, n + 1)
                        nc.vector.tensor_tensor(wolo[:, k], wo_raw[:, k], wohi[:, k].bitcast(F32),
                                                ALU.subtract).then_inc(wo_lo, 1)

                    def begin(fr):
                        lower_weights(0)
                        dve.wait_ge(extra_in, 48)
                        nc.vector.tensor_tensor(extra[:, 0, :], extra[:, 0, :], extra[:, 1, :], ALU.add).then_inc(extra_done, 1)
                        dve.wait_ge(extra_done, 1)
                        dve.wait_ge(txt0_in, 16)
                        for i in range(1, NT):
                            stats_of(0, i)
                        add_patches(0)
                        dve.wait_ge(patch_done, 2)
                        stats_of(0, 0)
                        dve.wait_ge(pads, 3)
                        mean_of(0, 0, NT)
                        lower_weights(1)
                        xhat_of(0, 0, 0, NT)
                        lower_weights(2)
                        for u in FIRST:
                            if u[0] == "xT":
                                lower_x(fr, [u[1]])
                                if u[1] == len(TURNS) - 1:
                                    add_patches(1)
                            elif u[0] == "V":
                                take_values(fr, [u])
                            elif u[0] == "S":
                                i = u[2]
                                if i == NT - 1:
                                    dve.wait_ge(mask_made, 2)
                                masked(fr, 0, i)
                                if i < NT - 1:
                                    shares(0, 0, i + 1)
                                if i == BY_DVE[0] - 1:
                                    norm_one(0, 0)
                                if i < NT - 1:
                                    lower_wo(DOWNWARD.index(i) - 1)
                            else:
                                lower_qk(fr, u[0], 0)
                        shares(0, 0, 0)
                        dve.wait_ge(patch_done, B)
                        dve.wait_ge(txt_in, 16 * (B - 1))

                    def body(b, fr, last):
                        for p in range(NPAIR):
                            more = p + 1 < NPAIR or not last
                            nxt = (p + 1) % NPAIR
                            if more and nxt:
                                lower_qk(fr, "Q", nxt)
                            take_turned(b, p, 0)
                            if more and nxt == 0:
                                lower_qk(fr, "Q", nxt)
                            if more:
                                lower_qk(fr, "K", nxt)
                            take_turned(b, p, 1)
                            if p < NT and not last:
                                stats_of(b + 1, p)
                            if p == NPAIR - 3 and not last:
                                mean_of(norm_no(b, 0), 0, NT)
                            if p == NPAIR - 2 and not last:
                                xhat_of(b + 1, norm_no(b, 0), 0, NT)
                            for j in range(NT):
                                if more:
                                    masked(fr, nxt, NT - 1 - j)
                                if j + 2 < NT:
                                    take_turned(b, p, j + 2)
                                if more and j + 3 < NT:
                                    shares(b, p + 1, NT - 1 - j)
                            if more:
                                shares(b, p + 1, 2)
                                norm_one(b, p + 1)
                                shares(b, p + 1, 1)
                            if more:
                                shares(b, p + 1, 0)
                            if p == NPAIR - 2 and not last:
                                lower_x(fr)

                        def lower_y(i):
                            dve.wait_ge(yhi_done, b * NT + i + 1)
                            nc.vector.tensor_tensor(ylo[i % 2][:, :, 0:SIZE[i]], yT[:, :, START[i]:START[i] + SIZE[i]],
                                                    yhi[i % 2][:, :, 0:SIZE[i]].bitcast(F32), ALU.subtract
                                                    ).then_inc(ylo_done, 1)

                        lower_y(0)
                        if not last:
                            take_values(fr, VALUES[:2])
                        lower_y(1)
                        if not last:
                            take_values(fr, VALUES[2:EARLY])
                        n = norm_no(b, 1, last)
                        for i in range(NT):
                            u = ("O", i)
                            dve.wait_ge(unit_ready, fr.is_ready(u))
                            nc.vector.tensor_tensor(h_tile(b, i), work[0:SIZE[i], fr.banks[u][0], 0:C], h_tile(b, i),
                                                    ALU.add).then_inc(unit_free, 1)
                            dve.wait_ge(unit_free, fr.is_free(u))
                            dve.sem_inc(passed_dve, 1)
                            stats_of(b, i)
                            if i + 2 < NT:
                                lower_y(i + 2)
                            if last and i >= NT - 2:
                                mean_of(n, 0 if i < NT - 1 else NT - 1, i + 1)
                        if last:
                            xhat_of(b, n, 0, NT - 1)
                            xhat_of(b, n, NT - 1, NT)
                        else:
                            mean_of(n, 0, NT)
                            take_values(fr, VALUES[EARLY:EARLY + 2])
                            xhat_of(b, n, 0, NT)
                        if not last:
                            take_values(fr, VALUES[EARLY + 2:])
                        for g in range(len(TURNS)):
                            u = ("x2T", g)
                            lo, hi = turned_tokens(g)
                            dve.wait_ge(unit_ready, fr.is_ready(u))
                            src = work[:, fr.banks[u][0], :].rearrange("p (c n) -> p c n", c=CC)[:, :, 0:hi - lo]
                            if g == 0:
                                dst = x2T[:, :, bass.ds(b * T0 + REST, T0)]
                            else:
                                dst = x2T[:, :, bass.ds(b * TXT + (lo - T0), hi - lo)]
                            nc.vector.tensor_copy(dst, src).then_inc(unit_free, 1)

                    batches(dve, begin, body)

        with ExitStack() as two:
            def sb(name, shape, dt=F32):
                return two.enter_context(nc.sbuf_tensor(name, shape, dt))

            x2hi = sb("x2hi", [128, CC, NTOK], F32R)
            x2lo = sb("x2lo", [128, CC, NTOK], F32R)
            fhi = sb("fhi", [128, 2, FT, 512], F32R)
            flo = sb("flo", [128, 2, FT, 512], F32R)
            silu = sb("silu", [128, 2, 512])
            fuse = sb("fuse", [128, 2, 512])
            mixed = sb("mixed", [128, 2, C])
            logitT = sb("logitT", [E, NTOK])
            logit = sb("logit", [128, ND, E])
            pr = sb("pr", [128, ND, E])
            eq = sb("eq", [128, ND, E])
            ahead = sb("ahead", [128, E])
            one_hot = sb("one_hot", [128, 2, ND, E])
            gatew = sb("gatew", [128, ND, E])
            wcol = sb("wcol", [128, 2, ND])
            r1 = sb("r1", [128, 8, ND])

            moved = sem("moved")
            x2_hi, x2_lo = sem("x2_hi"), sem("x2_lo")
            l_ready, l_done, l_zero, lt_ready, lt_done = (
                sem(n) for n in ("l_ready", "l_done", "l_zero", "lt_ready", "lt_done"))
            step = sem("step")
            ahead_made, x2_lo_rest = sem("ahead_made"), sem("x2_lo_rest")
            pair_asked, pair_given = sem("pair_asked"), sem("pair_given")
            exp_asked, exp_given = sem("exp_asked"), sem("exp_given")
            gu_ready, silu_done, fuse_done, fhi_done, flo_done = (
                sem(n) for n in ("gu_ready", "silu_done", "fuse_done", "fhi_done", "flo_done"))
            down_ready, down_done = sem("down_ready"), sem("down_done")
            wcol_done, stored = sem("wcol_done"), sem("stored")
            NC = len(CHUNKS)
            GU_AHEAD, DOWN_AHEAD = 1, 4
            NG = NC * FT
            SPLITS = [(c, lo, hi) for lo, hi in CHUNKS for c in range(CC)]
            dbanks = [turned[0], turned[1], y_text, y_first]

            def acc_of(k):
                if k < B * (NT - 1):
                    return acc[:, k, :]
                return mixed[0:DOWN[k][1], k - B * (NT - 1), :]

            with nc.Block() as block:
                def part(buf, s, what, *at):
                    if what == "down":
                        f = at[0]
                        o = 2 * CC * F + f * C
                        return buf[s][:, o:o + C]
                    c, f = at
                    o = (CC * F if what == "up" else 0) + c * F + f * 128
                    return buf[s][:, o:o + 128]

                @block.sync
                def _(sp):
                    for b in range(B):
                        dst = mixed[T0 * b:T0 * (b + 1), 0, :] if b < 3 else mixed[0:T0, 1, :]
                        sp.dma_start(dst, first[:, b, :]).then_inc(moved, 16)

                    with sp.Fori(0, E - 1) as e:
                        sp.wait_ge(we_lo, (e + 1) * len(PIECES))
                        load_expert(sp, e + 1)
                    last = (E - 1) * ND
                    order = [k for c in range(NC) for k in chunk_tiles(c)]
                    for n, k in enumerate(order):
                        sp.wait_ge(down_done, DOWN_AHEAD + last + n + 1)
                        if k < B * (NT - 1):
                            b, i = k // (NT - 1), k % (NT - 1)
                            sp.dma_start(out[b, T0 + 128 * i:T0 + 128 * i + 128, :], acc[:, k, :]).then_inc(stored, 16)
                        elif k == B * (NT - 1):
                            for b in range(3):
                                sp.dma_start(out[b, 0:T0, :], mixed[T0 * b:T0 * (b + 1), 0, :]).then_inc(stored, 16)
                        else:
                            sp.dma_start(out[3, 0:T0, :], mixed[0:T0, 1, :]).then_inc(stored, 16)
                    sp.wait_ge(stored, 16 * (B * (NT - 1) + B))

                def tiles_before(c):
                    return sum(len(chunk_tiles(k)) for k in range(c))

                def experts(eng, body):
                    with eng.Fori(0, E // 2 - 1) as pair:
                        for s in range(2):
                            body(pair * 2 + s, s, False)
                    for s in range(2):
                        body(E - 2 + s, s, s == 1)

                STEPS = [(c + 1, c) for c in range(NC - 1)] + [(NC, NC - 1)]

                @block.gpsimd
                def _(pool):
                    nc.gpsimd.memset(logit[:, :, :], 0.0).then_inc(l_zero, 1)
                    for k in range(E):
                        nc.gpsimd.memset(ahead[:, k:k + 1], float(E - k)).then_inc(ahead_made, 1)
                    for n in range(CC, len(SPLITS)):
                        c, lo, hi = SPLITS[n]
                        pool.wait_ge(x2_hi, n + 1)
                        nc.gpsimd.tensor_tensor(x2lo[:, c, lo:hi], x2T[:, c, lo:hi], x2hi[:, c, lo:hi].bitcast(F32),
                                                ALU.subtract).then_inc(x2_lo_rest, 1)
                @block.tensor
                def _(pe):
                    pe.sem_inc(down_ready, 1)
                    def logits(n):
                        lo, hi = CHUNKS[n]
                        if n >= 2:
                            pe.wait_ge(lt_done, n - 1)
                        for c in range(CC):
                            mm = nc.tensor.matmul(dbanks[2 + n % 2][0:E, 0:hi - lo], wr[:, c, :], x2T[:, c, lo:hi],
                                                  start=(c == 0), stop=(c == CC - 1))
                        mm.then_inc(lt_ready, 1)

                    def gate_up(e, s, c, f):
                        lo, hi = CHUNKS[c]
                        bank = 2 * ((c * FT + f) % 2)
                        if not (isinstance(e, int) and e == 0 and c * FT + f == 0):
                            pe.wait_ge(fuse_done, GU_AHEAD + e * NG + c * FT + f - 1)
                        for w, what in enumerate(("gate", "up")):
                            dst = work[:, bank + w, 0:hi - lo]
                            for k in range(CC):
                                wh, wl = part(wehi, s, what, k, f), part(welo, s, what, k, f)
                                xh, xl = x2hi[:, k, lo:hi], x2lo[:, k, lo:hi]
                                nc.tensor.matmul(dst, wh, xh, start=(k == 0), stop=False)
                                nc.tensor.matmul(dst, wh, xl, start=False, stop=False)
                                mm = nc.tensor.matmul(dst, wl, xh, start=False, stop=(k == CC - 1))
                        mm.then_inc(gu_ready, 1)

                    def down(e, s, c, t):
                        at, rows = DOWN[chunk_tiles(c)[t]]
                        off = at - CHUNKS[c][0]
                        n = tiles_before(c) + t
                        if t == 0:
                            pe.wait_ge(flo_done, e * NG + (c + 1) * FT)
                        pe.wait_ge(down_done, DOWN_AHEAD + e * ND + n - 3)
                        dst = dbanks[(s * ND + n) % 4][0:rows, 0:C]
                        for f in range(FT):
                            fh, fl = (x[:, (s * NC + c) % 2, f, off:off + rows] for x in (fhi, flo))
                            dh, dl = part(wehi, s, "down", f), part(welo, s, "down", f)
                            nc.tensor.matmul(dst, fh, dh, start=(f == 0), stop=False)
                            nc.tensor.matmul(dst, fh, dl, start=False, stop=False)
                            mm = nc.tensor.matmul(dst, fl, dh, start=False, stop=(f == FT - 1))
                        mm.then_inc(down_ready, 1)

                    def body(e, s, last):
                        for c, before in STEPS:
                            tiles = len(chunk_tiles(before))
                            if c == NC and last:
                                for t in range(tiles):
                                    down(e, s, before, t)
                                continue
                            if c == NC:
                                pe.wait_ge(we_lo, (e + 2) * len(PIECES))
                            nxt = (e + 1, 1 - s, 0) if c == NC else (e, s, c)
                            for f in range(FT):
                                gate_up(*nxt, f)
                                if f:
                                    down(e, s, before, f - 1)
                            for t in range(FT - 1, tiles):
                                down(e, s, before, t)

                    pe.wait_ge(wr_in, 16)
                    logits(0)
                    pe.wait_ge(we_lo, len(PIECES))
                    pe.wait_ge(x2_lo, CC)
                    for f in range(FT):
                        gate_up(0, 0, 0, f)
                        if f == 0:
                            for n in range(1, NC):
                                logits(n)
                        elif f == 1:
                            pe.wait_ge(lt_done, NC)
                            for k, (at, rows) in enumerate(DOWN):
                                mm = nc.tensor.transpose(turned[0][0:rows, k * E:k * E + E], logitT[:, at:at + rows],
                                                         ident[0:E, 0:E])
                            mm.then_inc(l_ready, 1)
                    pe.wait_ge(x2_lo_rest, len(SPLITS) - CC)
                    pe.wait_ge(l_done, 3)
                    experts(pe, body)

                @block.scalar
                def _(act):
                    def upper_x2(n):
                        c, lo, hi = SPLITS[n]
                        nc.scalar.activation(x2hi[:, c, lo:hi], x2T[:, c, lo:hi], ACT.Copy).then_inc(x2_hi, 1)

                    def gate(e, s, c, f):
                        n = c * FT + f
                        w = CHUNKS[c][1] - CHUNKS[c][0]
                        act.wait_ge(gu_ready, e * NG + n + 1)
                        nc.scalar.activation(silu[:, n % 2, 0:w], work[:, 2 * (n % 2), 0:w],
                                             ACT.Silu).then_inc(silu_done, 1)

                    def upper(e, s, c, f):
                        n = c * FT + f
                        w = CHUNKS[c][1] - CHUNKS[c][0]
                        act.wait_ge(fuse_done, GU_AHEAD + e * NG + n + 1)
                        nc.scalar.activation(fhi[:, (s * NC + c) % 2, f, 0:w], fuse[:, n % 2, 0:w],
                                             ACT.Copy).then_inc(fhi_done, 1)

                    def body(e, s, last):
                        for c, before in STEPS:
                            if c == NC and last:
                                upper(e, s, before, FT - 1)
                                continue
                            nxt = (e + 1, 1 - s, 0) if c == NC else (e, s, c)
                            for f in range(FT):
                                gate(*nxt, f)
                                if f == 0:
                                    upper(e, s, before, FT - 1)
                                    act.wait_ge(down_ready, 1 + e * ND + tiles_before(c - 1))
                                else:
                                    upper(*nxt, f - 1)
                                if c <= len(PIECES) // 2 and f % 2 and not last:
                                    split_upper(act, e + 1, 1 - s, 2 * (c - 1) + f // 2)

                    def take_logits(n):
                        lo, hi = CHUNKS[n]
                        act.wait_ge(lt_ready, n + 1)
                        nc.scalar.activation(logitT[:, lo:hi], dbanks[2 + n % 2][0:E, 0:hi - lo], ACT.Copy).then_inc(lt_done, 1)

                    for n in range(CC):
                        upper_x2(n)
                    for n in range(NC):
                        take_logits(n)
                        for k in range(CC * (n + 1), min(CC * (n + 2), len(SPLITS))):
                            upper_x2(k)
                    gate(0, 0, 0, 0)
                    gate(0, 0, 0, 1)
                    upper(0, 0, 0, 0)
                    act.wait_ge(exp_asked, 1)
                    nc.scalar.activation(pr[:, :, :], pr[:, :, :], ACT.Exp).then_inc(exp_given, 1)
                    gate(0, 0, 0, 2)
                    upper(0, 0, 0, 1)
                    gate(0, 0, 0, 3)
                    upper(0, 0, 0, 2)
                    act.wait_ge(pair_asked, 1)
                    nc.scalar.activation(r1[:, 6, :], r1[:, 2, :], ACT.Sigmoid, scale=-1.0)
                    nc.scalar.activation(r1[:, 7, :], r1[:, 2, :], ACT.Sigmoid).then_inc(pair_given, 1)
                    experts(act, body)

                @block.vector
                def _(dve):
                    dve.sem_inc(fuse_done, GU_AHEAD)
                    dve.sem_inc(down_done, DOWN_AHEAD)

                    def lower_x2(n):
                        c, lo, hi = SPLITS[n]
                        dve.wait_ge(x2_hi, n + 1)
                        nc.vector.tensor_tensor(x2lo[:, c, lo:hi], x2T[:, c, lo:hi], x2hi[:, c, lo:hi].bitcast(F32),
                                                ALU.subtract).then_inc(x2_lo, 1)

                    def fused(e, s, c, f):
                        n = c * FT + f
                        w = CHUNKS[c][1] - CHUNKS[c][0]
                        if not (isinstance(e, int) and e == 0 and n < 2):
                            dve.wait_ge(flo_done, e * NG + n - 1)
                        dve.wait_ge(silu_done, e * NG + n + 1)
                        nc.vector.tensor_tensor(fuse[:, n % 2, 0:w], work[:, 2 * (n % 2) + 1, 0:w],
                                                silu[:, n % 2, 0:w], ALU.mult).then_inc(fuse_done, 1)

                    def lower(e, s, c, f):
                        n = c * FT + f
                        w = CHUNKS[c][1] - CHUNKS[c][0]
                        fs = (s * NC + c) % 2
                        dve.wait_ge(fhi_done, e * NG + n + 1)
                        nc.vector.tensor_tensor(flo[:, fs, f, 0:w], fuse[:, n % 2, 0:w],
                                                fhi[:, fs, f, 0:w].bitcast(F32), ALU.subtract).then_inc(flo_done, 1)

                    def add(e, s, c, t):
                        k = chunk_tiles(c)[t]
                        rows = DOWN[k][1]
                        n = tiles_before(c) + t
                        dve.wait_ge(down_ready, 1 + e * ND + n + 1)
                        dst = acc_of(k)
                        nc.vector.scalar_tensor_tensor(out=dst, in0=dbanks[(s * ND + n) % 4][0:rows, 0:C],
                                                       scalar=wcol[0:rows, s, k:k + 1], in1=dst,
                                                       op0=ALU.mult, op1=ALU.add).then_inc(down_done, 1)

                    def body(e, s, last):
                        nc.vector.tensor_copy(wcol[:, s, :], gatew[:, :, bass.ds(e, 1)].rearrange("p k a -> p (k a)")
                                              ).then_inc(wcol_done, 1)
                        dve.wait_ge(wcol_done, e + 1)
                        for c, before in STEPS:
                            tiles = len(chunk_tiles(before))
                            if c == NC and last:
                                lower(e, s, before, FT - 1)
                                for t in range(tiles):
                                    add(e, s, before, t)
                                continue
                            nxt = (e + 1, 1 - s, 0) if c == NC else (e, s, c)
                            for f in range(FT):
                                fused(*nxt, f)
                                if f == 0:
                                    lower(e, s, before, FT - 1)
                                else:
                                    lower(*nxt, f - 1)
                                if c <= len(PIECES) // 2 and f % 2 and not last:
                                    split_lower(dve, e + 1, 1 - s, 2 * (c - 1) + f // 2)
                                if f >= 2:
                                    add(e, s, before, f - 2)
                            for t in range(FT - 2, tiles):
                                add(e, s, before, t)

                    links = [0]

                    def link(ins):
                        ins.then_inc(step, 1)
                        links[0] += 1
                        dve.wait_ge(step, links[0])

                    def spread(a):
                        return a.unsqueeze(2).to_broadcast([128, ND, E])

                    def ask_exp():
                        link(nc.vector.tensor_reduce(r1[:, 0, :], logit[:, :, :], AX.X, ALU.max))
                        nc.vector.tensor_tensor(pr[:, :, :], logit[:, :, :], spread(r1[:, 0, :]),
                                                ALU.subtract).then_inc(exp_asked, 1)

                    def highest(n, to):
                        link(nc.vector.tensor_reduce(r1[:, to, :], pr[:, :, :], AX.X, ALU.max))
                        link(nc.vector.tensor_tensor(eq[:, :, :], pr[:, :, :], spread(r1[:, to, :]), ALU.is_equal))
                        link(nc.vector.tensor_tensor(eq[:, :, :], eq[:, :, :],
                                                     ahead[:, :].unsqueeze(1).to_broadcast([128, ND, E]), ALU.mult))
                        link(nc.vector.tensor_reduce(r1[:, 7, :], eq[:, :, :], AX.X, ALU.max))
                        link(nc.vector.tensor_tensor(one_hot[:, n, :, :], eq[:, :, :], spread(r1[:, 7, :]), ALU.is_equal))

                    def first_expert():
                        dve.wait_ge(exp_given, 1)
                        link(nc.vector.tensor_reduce(r1[:, 7, :], pr[:, :, :], AX.X, ALU.add))
                        link(nc.vector.reciprocal(r1[:, 0, :], r1[:, 7, :]))
                        link(nc.vector.tensor_tensor(pr[:, :, :], pr[:, :, :], spread(r1[:, 0, :]), ALU.mult))
                        dve.wait_ge(ahead_made, E)
                        highest(0, 1)

                    def second_expert():
                        link(nc.vector.scalar_tensor_tensor(out=pr[:, :, :], in0=one_hot[:, 0, :, :], scalar=-2.0,
                                                            in1=pr[:, :, :], op0=ALU.mult, op1=ALU.add))
                        highest(1, 4)
                        nc.vector.tensor_tensor(r1[:, 2, :], r1[:, 4, :], r1[:, 1, :], ALU.subtract).then_inc(pair_asked, 1)

                    def weights_of_both():
                        dve.wait_ge(pair_given, 1)
                        link(nc.vector.tensor_tensor(gatew[:, :, :], one_hot[:, 0, :, :], spread(r1[:, 6, :]), ALU.mult))
                        link(nc.vector.tensor_tensor(eq[:, :, :], one_hot[:, 1, :, :], spread(r1[:, 7, :]), ALU.mult))
                        link(nc.vector.tensor_tensor(gatew[:, :, :], gatew[:, :, :], eq[:, :, :], ALU.add))

                    for n in range(CC):
                        lower_x2(n)
                    fused(0, 0, 0, 0)
                    fused(0, 0, 0, 1)
                    lower(0, 0, 0, 0)
                    dve.wait_ge(l_ready, 1)
                    dve.wait_ge(l_zero, 1)
                    full = B * (NT - 1)
                    bank = turned[0][:, 0:ND * E].rearrange("p (k e) -> p k e", e=E)
                    for rows, a, b in ((128, 0, full), (X_ROWS, full, full + 1), (T0, full + 1, ND)):
                        nc.vector.tensor_copy(logit[0:rows, a:b, :], bank[0:rows, a:b, :]).then_inc(l_done, 1)
                    dve.wait_ge(l_done, 3)
                    ask_exp()
                    first_expert()
                    fused(0, 0, 0, 2)
                    lower(0, 0, 0, 1)
                    second_expert()
                    fused(0, 0, 0, 3)
                    lower(0, 0, 0, 2)
                    weights_of_both()
                    dve.wait_ge(moved, 16 * B)
                    experts(dve, body)
    return nc


_INS = ["x", "txt", "L0_tok_W", "L0_tok_b", "L0_tok_cls_token", "L0_tok_pos_emb", "L0_attn_w_q", "L0_attn_w_k",
        "L0_attn_w_v", "L0_attn_w_o", "L0_ffn_kernel_router_DE", "L0_ffn_kernel_gating_EDF",
        "L0_ffn_kernel_up_EDF", "L0_ffn_kernel_down_EFD"]


def kernel(**inputs):
    import numpy as np
    import concourse.bacc as bacc
    from concourse.bass_utils import run_bass_kernel_spmd

    nc = bacc.Bacc("TRN2", target_bir_lowering=False, num_devices=1)
    arrays, args = {}, []
    for name in _INS:
        a = np.ascontiguousarray(inputs[name])
        arrays[f"in_{name}"] = a
        args.append(nc.dram_tensor(f"in_{name}", a.shape, mybir.dt.from_np(a.dtype), kind="ExternalInput").ap())
    args.append(nc.dram_tensor("out", (B, T, C), F32, kind="ExternalOutput").ap())
    fusion_block_kernel(nc, *args)
    r = run_bass_kernel_spmd(nc, [arrays], core_ids=[0])
    return r.results[0]["out"]
```
